# Optimizing a Trainium2 kernel written in Bass

```python
import numpy as np
import jax
import jax.numpy as jnp

def _softmax(x, axis=-1):
    return jax.nn.softmax(x, axis=axis)

def _gelu(x):
    return jax.nn.gelu(x, approximate=True)

def _silu(x):
    return jax.nn.silu(x)

def _sigmoid(x):
    return jax.nn.sigmoid(x)

def _layernorm(x, axis=-1, eps=1e-05):
    m = jnp.mean(x, axis=axis, keepdims=True)
    v = jnp.var(x, axis=axis, keepdims=True)
    return (x - m) / jnp.sqrt(v + eps)

def _scatter_add(tgt, idx, src, axis=0):
    return tgt.at[idx].add(src)

def _segment_sum(src, seg, n):
    return jax.ops.segment_sum(src, seg, n)
kernel_name = 'mk_macaron_d1_jaxref_r8_867f2d'

def setup_inputs(seed: int=0):
    np.random.seed(seed)
    _w = jnp.asarray

    def _L0_attn_setup():
        import jax, jax.numpy as jnp
        import numpy as np
        B, L, D = (2, 256, 128)
        H, HD = (16, 64)
        LD = 32
        key = jax.random.key(seed)
        ks = jax.random.split(key, 6)
        s = lambda fan_in: 1.0 / np.sqrt(fan_in)
        x_bld = jax.random.normal(ks[0], (B, L, D), dtype=jnp.float32)
        Wq = jax.random.normal(ks[1], (D, H, HD), dtype=jnp.float32) * s(D)
        Wkv_down = jax.random.normal(ks[2], (D, LD), dtype=jnp.float32) * s(D)
        Wk_up = jax.random.normal(ks[3], (LD, H, HD), dtype=jnp.float32) * s(LD)
        Wv_up = jax.random.normal(ks[4], (LD, H, HD), dtype=jnp.float32) * s(LD)
        Wout = jax.random.normal(ks[5], (H, HD, D), dtype=jnp.float32) * s(H * HD)
        return {'x_bld': x_bld, 'Wq': Wq, 'Wkv_down': Wkv_down, 'Wk_up': Wk_up, 'Wv_up': Wv_up, 'Wout': Wout}
    _L0_attn_in = _L0_attn_setup()

    def _L0_ffn_setup():
        import jax, jax.numpy as jnp
        import numpy as np
        INT4_QMAX = 7.0

        def simulate_quantize_int4(w):
            scale = jnp.max(jnp.abs(w)) / INT4_QMAX
            q = jnp.clip(jnp.round(w / scale), -8.0, 7.0)
            return q * scale
        key = jax.random.key(seed)
        k_x, k_w, k_bias, k_a, k_b = jax.random.split(key, 5)
        d_in, features, rank = (128, 128, 16)
        x = jax.random.normal(k_x, (4, 1024, d_in), dtype=jnp.float32)
        kernel = jax.random.normal(k_w, (d_in, features), dtype=jnp.float32)
        bias = jax.random.normal(k_bias, (features,), dtype=jnp.float32)
        a = jax.random.normal(k_a, (d_in, rank), dtype=jnp.float32) * (1.0 / np.sqrt(d_in))
        b = jax.random.normal(k_b, (rank, features), dtype=jnp.float32) * 0.01
        return {'x': x, 'kernel': kernel, 'bias': bias, 'a': a, 'b': b}
    _L0_ffn_in = _L0_ffn_setup()
    _d = {'L0_attn_x_bld': _L0_attn_in['x_bld'], 'L0_attn_Wq': _L0_attn_in['Wq'], 'L0_attn_Wkv_down': _L0_attn_in['Wkv_down'], 'L0_attn_Wk_up': _L0_attn_in['Wk_up'], 'L0_attn_Wv_up': _L0_attn_in['Wv_up'], 'L0_attn_Wout': _L0_attn_in['Wout'], 'L0_ffn_kernel': _L0_ffn_in['kernel'], 'L0_ffn_bias': _L0_ffn_in['bias'], 'L0_ffn_a': _L0_ffn_in['a'], 'L0_ffn_b': _L0_ffn_in['b']}
    _x0 = _d['L0_attn_x_bld']
    _d['L0_attn_x_bld'] = jax.random.normal(jax.random.fold_in(jax.random.key(seed), 1), (16, 512, 128), dtype=_x0.dtype)
    del _x0
    return _d

def reference(L0_attn_x_bld, L0_attn_Wq, L0_attn_Wkv_down, L0_attn_Wk_up, L0_attn_Wv_up, L0_attn_Wout, L0_ffn_kernel, L0_ffn_bias, L0_ffn_a, L0_ffn_b):

    def _L0_attn_ref(x_bld, Wq, Wkv_down, Wk_up, Wv_up, Wout):
        import jax, jax.numpy as jnp
        import numpy as np
        B, L, D = (2, 256, 128)
        H, HD = (16, 64)
        LD = 32
        q_blhd = jnp.einsum('bld,dhk->blhk', x_bld, Wq)
        latent_bll = jnp.einsum('bld,dc->blc', x_bld, Wkv_down)
        k_blhd = jnp.einsum('blc,chk->blhk', latent_bll, Wk_up)
        v_blhd = jnp.einsum('blc,chk->blhk', latent_bll, Wv_up)
        attn = jnp.einsum('bqhd,bkhd->bhqk', q_blhd, k_blhd) / jnp.sqrt(jnp.asarray(HD, dtype=x_bld.dtype))
        l = x_bld.shape[1]
        mask = (jnp.arange(l)[None, :] <= jnp.arange(l)[:, None])[None, None]
        neg_inf = jnp.finfo(attn.dtype).min
        attn = jax.nn.softmax(jnp.where(mask, attn, neg_inf), axis=-1)
        y_blhd = jnp.einsum('bhqk,bkhd->bqhd', attn, v_blhd)
        return jnp.einsum('bqhd,hdo->bqo', y_blhd, Wout)

    def _L0_ffn_ref(x, kernel, bias, a, b):
        import jax, jax.numpy as jnp
        import numpy as np
        INT4_QMAX = 7.0

        def simulate_quantize_int4(w):
            scale = jnp.max(jnp.abs(w)) / INT4_QMAX
            q = jnp.clip(jnp.round(w / scale), -8.0, 7.0)
            return q * scale
        w = simulate_quantize_int4(kernel)
        y = jnp.einsum('bsd,df->bsf', x, w) + bias
        lora = jnp.einsum('bsr,rf->bsf', jnp.einsum('bsd,dr->bsr', x, a), b)
        return y + lora
    x = L0_attn_x_bld
    x = x + 0.5 * _L0_ffn_ref(_layernorm(x, axis=-1), L0_ffn_kernel, L0_ffn_bias, L0_ffn_a, L0_ffn_b)
    x = x + _L0_attn_ref(_layernorm(x, axis=-1), L0_attn_Wq, L0_attn_Wkv_down, L0_attn_Wk_up, L0_attn_Wv_up, L0_attn_Wout)
    x = x + 0.5 * _L0_ffn_ref(_layernorm(x, axis=-1), L0_ffn_kernel, L0_ffn_bias, L0_ffn_a, L0_ffn_b)
    return x

_drawn_inputs = setup_inputs


def setup_inputs(seed=0):
    import zlib

    import numpy as np

    out = dict(_drawn_inputs(seed))
    spreads = {}
    factors = {'L0_ffn_a': 8.0, 'L0_ffn_b': 8.0}
    for name, (base, spread) in spreads.items():
        noise = np.random.default_rng([zlib.crc32(name.encode()), seed]).standard_normal(out[name].shape)
        drawn = base * np.exp(spread * noise) if base else spread * noise
        out[name] = jnp.asarray(drawn.astype(out[name].dtype))
    for name, factor in factors.items():
        out[name] = (out[name] * factor).astype(out[name].dtype)
    return out
```

```python
from contextlib import ExitStack

import concourse.bass as bass
from concourse import mybir

F32 = mybir.dt.float32
F32R = mybir.dt.float32r
ALU = mybir.AluOpType
ACT = mybir.ActivationFunctionType
AX = mybir.AxisListType

P = 128
B, L, D = 16, 512, 128
H, HD, LD = 16, 64, 32
RANK = 16
TT = L // P
HG = P // LD
G = H // HG
EPS = 1e-5
QMAX = 7.0
MASKED = -3.0e38
ROUND = 1.5 * 2.0 ** 23
KS = 3 * LD
KM = KS + 1

F_UNITS = 9
HALF = H // 2
PAIRS = HALF // 2 * TT
A_UNITS = 2 * (PAIRS + 1)
T_UNITS = 3
STEPS = G * TT
SCORES = STEPS * HG
DMA = 16
Q_DMAS = 3 * HG


def wait_batch(eng, sem, t, off, per, k):
    if isinstance(t, int):
        if t * per + off * per + k > 0:
            eng.wait_ge(sem, t * per + off * per + k)
    else:
        eng.wait_ge(sem, t * per + (off * per + k))


def nth(par):
    return DMA // 2, DMA - DMA // 2 * par


def units_of(s):
    first, n = 2, STEPS - 2
    return [] if s < first else list(range((s - first) * A_UNITS // n, (s - first + 1) * A_UNITS // n))


def macaron_block(nc, x, wq, wkv_down, wk_up, wv_up, wout, ffn_w, ffn_bias, ffn_a, ffn_b, out):
    ctx = ExitStack()
    with ctx:
        def sb(name, shape, dt=F32):
            return ctx.enter_context(nc.sbuf_tensor(name, shape, dt))

        def sem(name):
            return ctx.enter_context(nc.semaphore(name))

        x_tiles = x.rearrange("b (i p) d -> b p i d", p=P)
        out_tiles = out.rearrange("b (i p) d -> b p i d", p=P)

        wq_in = sb("wq_in", [P, H * HD])
        wk_in = sb("wk_in", [LD, H * HD])
        wv_in = sb("wv_in", [LD, H * HD])
        wout_in = sb("wout_in", [P, H // 2, D])
        wkv3 = sb("wkv3", [P, 3, LD])
        ffn_in = sb("ffn_in", [P, D])
        a_in = sb("a_in", [P, RANK])
        b_in = sb("b_in", [RANK, D])
        half_bias = sb("half_bias", [P, D])
        identity = sb("identity", [P, P])
        ones = sb("ones", [P, P])
        neg_half = sb("neg_half", [P, TT])
        corner = sb("corner", [P, 2, P])
        wq_t = sb("wq_t", [P, H // 2, D])
        wk_t = sb("wk_t", [P, H // 2, LD])
        wv_t = sb("wv_t", [P, H // 2, LD])
        a_t = sb("a_t", [RANK, P])
        w_query = sb("w_query", [P, H // 2, 2, LD])
        w_out = sb("w_out", [P, G, D])
        w_ffn = sb("w_ffn", [P, D])
        absmax = sb("absmax", [P, 4])
        quant = sb("quant", [P, 2, D])

        x_in = sb("x_in", [P, 2, TT, D])
        xb = sb("xb", [P, TT, D])
        x1 = sb("x1", [P, 2, TT, D])
        x1_back = sb("x1_back", [P, TT, D])
        x2 = sb("x2", [P, TT, D])
        x2b = sb("x2b", [P, TT, D])
        x3 = sb("x3", [P, TT, D])
        f_stats = sb("f_stats", [P, 2, TT, 6])
        f_mv = sb("f_mv", [P, 2, TT, 2])
        f_var = sb("f_var", [P, 2, TT])
        f_rstd = sb("f_rstd", [P, 2, TT])
        t_stats = sb("t_stats", [P, TT, 6])
        t_mv = sb("t_mv", [P, TT, 2])
        t_var = sb("t_var", [P, TT])
        t_rstd = sb("t_rstd", [P, TT])
        xn = sb("xn", [P, TT, D])
        xn_t = sb("xn_t", [P, L])
        xn3 = sb("xn3", [P, TT, D])
        xn3_t = sb("xn3_t", [P, L])
        q_high = sb("q_high", [P, G, L], F32R)
        q_low = sb("q_low", [P, G, L], F32R)
        lat_staged = sb("lat_staged", [P, TT, LD])
        keys_staged = sb("keys_staged", [KS, L], F32R)
        q_stack = [sb(f"q_stack{i}", [KM, H, L], F32R) for i in range(2)]
        keys = [sb(f"keys{i}", [KM, L], F32R) for i in range(2)]
        lat = [sb(f"lat{i}", [P, TT, LD]) for i in range(2)]
        neg_max = sb("neg_max", [P, H * TT])
        neg_max_t = [sb(f"neg_max_t{i}", [HALF * TT, P], F32R) for i in range(2)]
        probs = [sb(f"probs{i}", [P, HG, L]) for i in range(2)]
        den_inv = sb("den_inv", [P, L])
        y_norm = sb("y_norm", [P, G, L])

        banks = [ctx.enter_context(nc.psum_tensor(f"bank{i}", [P, L], F32)) for i in range(2, 8)]
        pair = ctx.enter_context(nc.psum_tensor("pair", [P, 2, L], F32))
        front, tail, score0, score1, y_bank, den_bank = banks
        scores = [score0, score1]

        w_loaded = sem("w_loaded")
        const_made = sem("const_made")
        w_pe = sem("w_pe")
        w_dve = sem("w_dve")
        w_chain = sem("w_chain")
        x_loaded = [sem("x_loaded0"), sem("x_loaded1")]
        xb_made = sem("xb_made")
        f_dve = sem("f_dve")
        f_moments = sem("f_moments")
        f_pool = sem("f_pool")
        f_rstd_made = sem("f_rstd_made")
        f_normed = sem("f_normed")
        f_full = sem("f_full")
        f_free = sem("f_free")
        qh_made = sem("qh_made")
        kh_made = sem("kh_made")
        x1_saved = [sem("x1_saved0"), sem("x1_saved1")]
        x1_loaded = sem("x1_loaded")
        q_stacked = [sem("q_stacked0"), sem("q_stacked1")]
        keys_landed = sem("keys_landed")
        lat_landed = sem("lat_landed")
        a_full = sem("a_full")
        a_masked = sem("a_masked")
        a_free = sem("a_free")
        max_landed = [sem("max_landed0"), sem("max_landed1")]
        s_full = sem("s_full")
        exp_done = sem("exp_done")
        p_ready = sem("p_ready")
        pv_done = sem("pv_done")
        y_inv = sem("y_inv")
        y_free = sem("y_free")
        t_dve = sem("t_dve")
        t_moments = sem("t_moments")
        t_pool = sem("t_pool")
        t_rstd_made = sem("t_rstd_made")
        x2b_made = sem("x2b_made")
        t_normed = sem("t_normed")
        t_full = sem("t_full")
        t_free = sem("t_free")
        out_stored = sem("out_stored")
        waits_passed = sem("waits_passed")

        def wait_batch_alone(eng, sem, t, off, per, k):
            wait_batch(eng, sem, t, off, per, k)
            eng.sem_inc(waits_passed, 1)

        def stages(t):
            known = isinstance(t, int)
            return [not known or 0 <= t + off < B for off in (0, 1, 2, -1)]

        LOOP_FROM, LOOP_TO = 2, B - 4

        def rounds(eng, one_round):
            for t in range(-2, LOOP_FROM):
                one_round(t, t % 2)
            with eng.Fori(LOOP_FROM, LOOP_TO, 2) as t:
                one_round(t, 0)
                one_round(t + 1, 1)
            for t in range(LOOP_TO, B + 1):
                one_round(t, t % 2)

        block = ctx.enter_context(nc.Block())

        @block.sync
        def _(sp):
            for dst, src in (
                (wq_in[:], wq.rearrange("d h k -> d (h k)")),
                (wk_in[:], wk_up.rearrange("c h k -> c (h k)")),
                (wv_in[:], wv_up.rearrange("c h k -> c (h k)")),
                (wout_in[:], wout.rearrange("(g e) k o -> (e k) g o", e=2)),
                (ffn_in[:], ffn_w), (a_in[:], ffn_a), (b_in[:], ffn_b),
                (wkv3[:, 0, :], wkv_down), (wkv3[:, 1, :], wkv_down), (wkv3[:, 2, :], wkv_down),
                (half_bias[:], ffn_bias.rearrange("(o f) -> o f", o=1).broadcast_to([P, D])),
            ):
                sp.dma_start(dst, src).then_inc(w_loaded, DMA)
            sp.dma_start(x_in[:, 0], x_tiles[0]).then_inc(x_loaded[0], DMA)

            def one_round(t, par):
                attend, top, prep, end = stages(t)
                if end:
                    wait_batch_alone(sp, x1_saved[1 - par], t, -1, *nth(1 - par))
                    wait_batch_alone(sp, t_free, t, -2, T_UNITS, 1)
                    sp.dma_start(x1_back[:], out_tiles[t - 1]).then_inc(x1_loaded, DMA)
                if not isinstance(t, int) or t + 3 < B:
                    wait_batch_alone(sp, f_normed, t, 1, 2, 1)
                    wait_batch_alone(sp, xb_made, t, 1, 1, 1)
                    sp.dma_start(x_in[:, 1 - par], x_tiles[t + 3]).then_inc(x_loaded[1 - par], DMA)
                if prep:
                    wait_batch_alone(sp, f_free, t, 2, F_UNITS, 2)
                    sp.dma_start(out_tiles[t + 2], x1[:, par]).then_inc(x1_saved[par], DMA)
                if end:
                    wait_batch_alone(sp, t_free, t, -1, T_UNITS, 3)
                    sp.dma_start(out_tiles[t - 1], x3[:]).then_inc(out_stored, DMA)

                def stack_queries(half):
                    wait_batch_alone(sp, f_free, t, 2, F_UNITS, 3 + 2 * (half + 1))
                    wait_batch_alone(sp, s_full, t, 0, SCORES, SCORES // 2 * (half + 1))
                    g0 = 2 * half
                    for e in range(HG):
                        for part, src in enumerate((q_high, q_high, q_low)):
                            dst = q_stack[par][part * LD:(part + 1) * LD, g0 * HG:(g0 + 2) * HG, :]
                            dst = dst.rearrange("c (g e) l -> c g e l", e=HG)[:, :, e, :]
                            sp.dma_start(dst.bitcast(F32), src[e * LD:(e + 1) * LD, g0:g0 + 2, :].bitcast(F32)).then_inc(q_stacked[half], DMA)

                def place_max(half):
                    wait_batch_alone(sp, a_free, t, 1, A_UNITS, (half + 1) * (PAIRS + 1))
                    dst = q_stack[1 - par][KS:KM, half * HALF:(half + 1) * HALF, :].rearrange("o h (i q) -> o (h i) q", q=P)
                    sp.dma_start(dst.bitcast(F32), neg_max_t[half][:].bitcast(F32)).then_inc(max_landed[half], DMA)

                if prep:
                    stack_queries(0)
                if top:
                    place_max(0)
                if prep:
                    wait_batch_alone(sp, f_free, t, 2, F_UNITS, 8)
                    wait_batch_alone(sp, s_full, t, 0, SCORES, SCORES)
                    sp.dma_start(keys[par][0:KS, :].bitcast(F32), keys_staged[:].bitcast(F32)).then_inc(keys_landed, DMA)
                    stack_queries(1)
                    wait_batch_alone(sp, f_free, t, 2, F_UNITS, 9)
                    wait_batch_alone(sp, pv_done, t, 0, STEPS, STEPS)
                    sp.dma_start(lat[par][:], lat_staged[:]).then_inc(lat_landed, DMA)
                if top:
                    place_max(1)

            rounds(sp, one_round)
            sp.wait_ge(out_stored, DMA * B)
            for saved in x1_saved:
                sp.wait_ge(saved, DMA * B // 2)

        @block.gpsimd
        def _(pool):
            nc.gpsimd.memset(identity[:], 0.0).then_inc(const_made, 1)
            nc.gpsimd.memset(ones[:], 1.0).then_inc(const_made, 1)
            nc.gpsimd.memset(neg_half[:], -0.5).then_inc(const_made, 1)
            nc.gpsimd.memset(corner[:], 0.0).then_inc(const_made, 1)
            pool.wait_ge(const_made, 6)
            nc.gpsimd.affine_select(out=identity[:], in_=identity[:], compare_op=ALU.not_equal, fill=1.0, base=0,
                                    pattern=[[-1, P]], channel_multiplier=1).then_inc(const_made, 1)
            nc.gpsimd.affine_select(out=corner[:], in_=corner[:], compare_op=ALU.is_ge, fill=MASKED, base=0,
                                    pattern=[[0, 2], [-1, P]], channel_multiplier=1).then_inc(const_made, 1)
            pool.wait_ge(w_dve, 1)

            def one_round(t, par):
                attend, top, prep, end = stages(t)

                def rstd(moments, per, k, off, mv, var, out_, chain, done):
                    wait_batch_alone(pool, moments, t, off, per, k)
                    nc.gpsimd.tensor_scalar(var, mv, EPS, None, ALU.add).then_inc(chain, 1)
                    wait_batch(pool, chain, t, off, per, k)
                    nc.gpsimd.tensor_tensor(out_, var, neg_half[:], ALU.pow).then_inc(done, 1)

                for s in range(STEPS):
                    if prep and s == 0:
                        wait_batch(pool, x_loaded[par], t, 2, *nth(par))
                        wait_batch(pool, f_free, t, 1, F_UNITS, 2)
                        nc.gpsimd.tensor_tensor(xb[:], x_in[:, par], half_bias[:, None, :].broadcast_to([P, TT, D]),
                                                ALU.add).then_inc(xb_made, 1)
                        rstd(f_moments, 2, 1, 2, f_mv[:, 0, :, 1], f_var[:, 0], f_rstd[:, 0], f_pool, f_rstd_made)
                    if attend:
                        n = min(P, L)
                        wait_batch_alone(pool, exp_done, t, 0, SCORES, HG * (s + 1))
                        diag = probs[s % 2][:, :, 0:n]
                        nc.gpsimd.affine_select(out=diag, in_=diag, compare_op=ALU.is_ge, fill=0.0, base=0,
                                                pattern=[[0, HG], [1, n]], channel_multiplier=-1).then_inc(p_ready, 1)
                    if end and s == 1:
                        rstd(t_moments, 1, 1, -1, t_mv[:, :, 1], t_var[:], t_rstd[:], t_pool, t_rstd_made)
                    if prep and s == 2:
                        rstd(f_moments, 2, 2, 2, f_mv[:, 1, :, 1], f_var[:, 1], f_rstd[:, 1], f_pool, f_rstd_made)
                    if end and s == 3:
                        wait_batch(pool, t_free, t, -1, T_UNITS, 1)
                        nc.gpsimd.tensor_tensor(x2b[:], x2[:], half_bias[:, None, :].broadcast_to([P, TT, D]),
                                                ALU.add).then_inc(x2b_made, 1)

            rounds(pool, one_round)

        @block.scalar
        def _(act):
            def one_round(t, par):
                attend, top, prep, end = stages(t)

                def exp(s, e):
                    n = L - P * (s % TT)
                    u = HG * s + e
                    wait_batch(act, s_full, t, 0, SCORES, u + 1)
                    if e == 0:
                        wait_batch(act, pv_done, t, 0, STEPS, s - 1)
                    nc.scalar.activation(probs[s % 2][:, e, 0:n], scores[u % 2][:, 0:n], ACT.Exp).then_inc(exp_done, 1)

                for s in range(STEPS):
                    if attend:
                        exp(s, 0)
                        exp(s, 1)
                    if top:
                        for v in units_of(s):
                            half, i = divmod(v, PAIRS + 1)
                            if i == PAIRS:
                                wait_batch(act, a_full, t, 1, A_UNITS, v + 1)
                                wait_batch(act, max_landed[half], t, 1, DMA, 0)
                                nc.scalar.activation(neg_max_t[half][:], pair[0:HALF * TT, 0, 0:P],
                                                     ACT.Copy).then_inc(a_free, 1)
                    if attend:
                        exp(s, 2)
                        exp(s, 3)
                    if end and s == 3:
                        wait_batch(act, t_full, t, -1, T_UNITS, 2)
                        nc.scalar.activation(xn3_t[:], tail[:], ACT.Copy).then_inc(t_free, 1)
                    if prep:
                        if s in (1, 4):
                            wait_batch(act, f_full, t, 2, F_UNITS, 1 if s == 1 else 3)
                            nc.scalar.activation(xn_t[:], front[:], ACT.Copy).then_inc(f_free, 1)
                        if 5 <= s < 5 + G:
                            g = s - 5
                            wait_batch(act, f_full, t, 2, F_UNITS, 4 + g)
                            wait_batch(act, q_stacked[g // 2], t, 2, Q_DMAS * DMA, 0)
                            nc.scalar.activation(q_high[:, g, :], front[:], ACT.Copy).then_inc(qh_made, 1)
                        if s == 9:
                            wait_batch(act, f_full, t, 2, F_UNITS, 8)
                            wait_batch(act, keys_landed, t, 2, DMA, 0)
                            nc.scalar.activation(keys_staged[:], front[0:KS, :], ACT.Copy).then_inc(kh_made, 1)
                        if s == 10:
                            wait_batch(act, f_full, t, 2, F_UNITS, 9)
                            wait_batch(act, lat_landed, t, 2, DMA, 0)
                            nc.scalar.activation(lat_staged[:].rearrange("p i c -> p (i c)"), front[:, 0:TT * LD],
                                                 ACT.Copy).then_inc(f_free, 1)

            rounds(act, one_round)

        @block.tensor
        def _(pe):
            pe.wait_ge(w_loaded, 11 * DMA)
            pe.wait_ge(const_made, 8)
            for j in range(H // 2):
                nc.tensor.transpose(pair[:, j // 4, (j % 4) * P:(j % 4 + 1) * P], wq_in[:, j * P:(j + 1) * P], identity[:])
                nc.tensor.transpose(front[:, j * LD:(j + 1) * LD], wk_in[:, j * P:(j + 1) * P], identity[0:LD, 0:LD])
                nc.tensor.transpose(tail[:, j * LD:(j + 1) * LD], wv_in[:, j * P:(j + 1) * P], identity[0:LD, 0:LD])
            nc.tensor.transpose(score0[0:RANK, 0:P], a_in[:], identity[:]).then_inc(w_pe, 1)
            pe.wait_ge(w_dve, 2)
            nc.tensor.transpose(score1[0:1, 0:P], absmax[:, 0:1], identity[:]).then_inc(w_pe, 1)
            nc.tensor.matmul(score0[:, 0:D], a_t[:], b_in[:], start=True, stop=True)
            for odd, (q_bank, o_bank) in enumerate(((front, y_bank), (tail, den_bank))):
                rows = slice(odd * HD, (odd + 1) * HD)
                for j in range(H // 2):
                    e, g = (2 * j + odd) % HG, (2 * j + odd) // HG
                    nc.tensor.matmul(q_bank[:, j * LD:(j + 1) * LD], wq_t[rows, j, :], wk_t[rows, j, :],
                                     start=True, stop=True)
                    last = nc.tensor.matmul(o_bank[e * LD:(e + 1) * LD, g * D:(g + 1) * D], wv_t[rows, j, :],
                                            wout_in[rows, j, :], start=True, stop=True)
            last.then_inc(w_pe, 1)
            pe.wait_ge(w_dve, 3)
            nc.tensor.matmul(score1[:, 0:1], ones[0:1, :], absmax[0:1, 2:3], start=True, stop=True).then_inc(w_pe, 1)
            pe.wait_ge(w_dve, 4)

            def one_round(t, par):
                attend, top, prep, end = stages(t)

                def score(s, e):
                    g, j = divmod(s, TT)
                    u = HG * s + e
                    if e == 0 and j == 0 and g % 2 == 0:
                        wait_batch(pe, max_landed[g // 2], t, 0, DMA, DMA)
                    wait_batch(pe, exp_done, t, 0, SCORES, u - 1)
                    nc.tensor.matmul(scores[u % 2][:, 0:L - P * j], keys[par][:, j * P:(j + 1) * P],
                                     q_stack[par][:, g * HG + e, j * P:L], start=True, stop=True).then_inc(s_full, 1)

                def weigh(s, bank, weights, ready):
                    g, j = divmod(s, TT)
                    if ready:
                        wait_batch(pe, p_ready, t, 0, STEPS, s + 1)
                        if s == 0:
                            wait_batch(pe, lat_landed, t, 0, DMA, DMA)
                        if j == 0:
                            wait_batch(pe, y_free, t, 0, G, g)
                    for e in range(HG):
                        last = nc.tensor.matmul(bank[e * LD:(e + 1) * LD, j * P:L], weights,
                                                probs[s % 2][:, e, 0:L - P * j], start=(j == 0), stop=(j == TT - 1))
                    return last

                def weigh_latents(s):
                    weigh(s, y_bank, lat[par][:, s % TT, :], True)

                def weigh_ones(s):
                    weigh(s, den_bank, ones[:, 0:LD], False).then_inc(pv_done, 1)

                def max_unit(v):
                    half, i = divmod(v, PAIRS + 1)
                    wait_batch(pe, a_free, t, 1, A_UNITS, v)
                    if i == PAIRS:
                        nc.tensor.transpose(pair[0:HALF * TT, 0, 0:P], neg_max[:, half * HALF * TT:(half + 1) * HALF * TT],
                                            identity[:]).then_inc(a_full, 1)
                        return
                    if i == 0:
                        wait_batch(pe, q_stacked[half], t, 1, Q_DMAS * DMA, Q_DMAS * DMA)
                        if half == 0:
                            wait_batch(pe, keys_landed, t, 1, DMA, DMA)
                    h, j = half * HALF + 2 * (i // TT), i % TT
                    n = P * (j + 1)
                    for k in range(2):
                        last = nc.tensor.matmul(pair[:, k, 0:n], q_stack[1 - par][0:KS, h + k, j * P:(j + 1) * P],
                                                keys[1 - par][0:KS, 0:n], start=True, stop=True)
                    last.then_inc(a_full, 1)

                def front_unit(u):
                    wait_batch(pe, f_free, t, 2, F_UNITS, u)
                    if u in (0, 2):
                        wait_batch(pe, f_normed, t, 2, 2, 1 + u // 2)
                        for i in range(TT):
                            last = nc.tensor.transpose(front[:, i * P:(i + 1) * P], xn[:, i, :], identity[:])
                    elif u == 1:
                        for i in range(TT):
                            last = nc.tensor.matmul(front[:, i * D:(i + 1) * D], xn_t[:, i * P:(i + 1) * P], w_ffn[:],
                                                    start=True, stop=True)
                    elif u < 7:
                        w = w_query[:, 2 * (u - 3):2 * (u - 2)].rearrange("p j e c -> p (j e c)")
                        last = nc.tensor.matmul(front[:], w, xn_t[:], start=True, stop=True)
                    elif u == 7:
                        last = nc.tensor.matmul(front[0:KS, :], wkv3[:].rearrange("p r c -> p (r c)"), xn_t[:],
                                                start=True, stop=True)
                    else:
                        for i in range(TT):
                            last = nc.tensor.matmul(front[:, i * LD:(i + 1) * LD], xn_t[:, i * P:(i + 1) * P],
                                                    wkv3[:, 0, :], start=True, stop=True)
                    last.then_inc(f_full, 1)

                def tail_unit(u):
                    wait_batch(pe, t_free, t, -1, T_UNITS, u)
                    if u == 0:
                        wait_batch(pe, y_free, t, -1, G, G)
                        for i in range(TT):
                            for g in range(G):
                                last = nc.tensor.matmul(tail[:, i * D:(i + 1) * D], y_norm[:, g, i * P:(i + 1) * P],
                                                        w_out[:, g, :], start=(g == 0), stop=(g == G - 1))
                    elif u == 1:
                        wait_batch(pe, t_normed, t, -1, 1, 1)
                        for i in range(TT):
                            last = nc.tensor.transpose(tail[:, i * P:(i + 1) * P], xn3[:, i, :], identity[:])
                    else:
                        for i in range(TT):
                            last = nc.tensor.matmul(tail[:, i * D:(i + 1) * D], xn3_t[:, i * P:(i + 1) * P], w_ffn[:],
                                                    start=True, stop=True)
                    last.then_inc(t_full, 1)

                for s in range(STEPS):
                    if attend:
                        score(s, 0)
                        score(s, 1)
                    if top:
                        for v in units_of(s):
                            max_unit(v)
                    if attend:
                        score(s, 2)
                        if s:
                            weigh_latents(s - 1)
                        score(s, 3)
                        if s:
                            weigh_ones(s - 1)
                    if end and s in (1, 3, 4):
                        tail_unit((1, 3, 4).index(s))
                    if prep and s in (1, 2) or prep and 4 <= s < 11:
                        front_unit(s - 1 if s < 3 else s - 2)
                if attend:
                    weigh_latents(STEPS - 1)
                    weigh_ones(STEPS - 1)

            rounds(pe, one_round)

        @block.vector
        def _(dve):
            nc.vector.memset(keys[0][KS:KM, :].bitcast(F32), 1.0).then_inc(const_made, 1)
            nc.vector.memset(keys[1][KS:KM, :].bitcast(F32), 1.0).then_inc(const_made, 1)
            dve.wait_ge(w_loaded, 11 * DMA)
            nc.vector.tensor_scalar(half_bias[:], half_bias[:], 0.5, None, ALU.mult).then_inc(w_dve, 1)
            nc.vector.tensor_reduce(absmax[:, 0:1], ffn_in[:], AX.X, ALU.max, apply_absolute_value=True)
            dve.wait_ge(w_pe, 1)
            nc.vector.tensor_copy(wq_t[:].rearrange("p (a j) d -> p a (j d)", a=2), pair[:])
            nc.vector.tensor_copy(wk_t[:].rearrange("p j c -> p (j c)"), front[:, 0:H // 2 * LD])
            nc.vector.tensor_copy(wv_t[:].rearrange("p j c -> p (j c)"), tail[:, 0:H // 2 * LD])
            nc.vector.tensor_copy(a_t[:], score0[0:RANK, 0:P]).then_inc(w_dve, 1)
            dve.wait_ge(w_pe, 2)
            chain = [0]

            def link(ins):
                chain[0] += 1
                ins.then_inc(w_chain, 1)
                dve.wait_ge(w_chain, chain[0])

            link(nc.vector.tensor_reduce(absmax[0:1, 1:2], score1[0:1, 0:P], AX.X, ALU.max))
            nc.vector.tensor_scalar(absmax[0:1, 2:3], absmax[0:1, 1:2], 1.0 / QMAX, None, ALU.mult).then_inc(w_dve, 1)
            dve.wait_ge(w_pe, 3)
            for odd, (q_bank, o_bank) in enumerate(((front, y_bank), (tail, den_bank))):
                nc.vector.tensor_scalar(w_query[:, :, odd, :], q_bank[:, 0:H // 2 * LD].rearrange("p (j c) -> p j c", c=LD),
                                        HD ** -0.5, None, ALU.mult)
                for e in (odd, odd + 2):
                    rows = slice(e * LD, (e + 1) * LD)
                    nc.vector.tensor_copy(w_out[rows].rearrange("p g o -> p (g o)"), o_bank[rows, :])
            dve.wait_ge(w_pe, 4)
            link(nc.vector.tensor_copy(absmax[:, 3:4], score1[:, 0:1]))
            link(nc.vector.reciprocal(absmax[:, 1:2], absmax[:, 3:4]))
            link(nc.vector.tensor_scalar(quant[:, 0], ffn_in[:], absmax[:, 1:2], ROUND, ALU.mult, ALU.add))
            link(nc.vector.tensor_scalar(quant[:, 1], quant[:, 0], -ROUND, QMAX, ALU.add, ALU.min))
            link(nc.vector.tensor_scalar(quant[:, 0], quant[:, 1], -QMAX - 1.0, absmax[:, 3:4], ALU.max, ALU.mult))
            link(nc.vector.tensor_tensor(quant[:, 1], score0[:, 0:D], quant[:, 0], ALU.add))
            nc.vector.tensor_scalar(w_ffn[:], quant[:, 1], 0.5, None, ALU.mult).then_inc(w_dve, 1)

            def one_round(t, par):
                attend, top, prep, end = stages(t)

                def moments(src, stats, mv, chain, per, k, off, done):
                    for i in range(TT):
                        last = nc.vector.bn_stats(stats[:, i, :], src[:, i, :])
                    last.then_inc(chain, 1)
                    wait_batch_alone(dve, chain, t, off, per, k)
                    for i in range(TT):
                        last = nc.vector.bn_aggr(mv[:, i, :], stats[:, i, :])
                    last.then_inc(done, 1)

                def normalise(dst, src, mv, rstd):
                    for i in range(TT):
                        last = nc.vector.tensor_scalar(dst[:, i, :], src[:, i, :], mv[:, i, 0:1], rstd[:, i:i + 1],
                                                       ALU.subtract, ALU.mult)
                    return last

                def max_unit(v):
                    half, i = divmod(v, PAIRS + 1)
                    if i == PAIRS:
                        return
                    h, j = half * HALF + 2 * (i // TT), i % TT
                    n = P * (j + 1)
                    k0 = n - P
                    wait_batch(dve, a_full, t, 1, A_UNITS, v + 1)
                    nc.vector.tensor_tensor(pair[:, :, k0:n], pair[:, :, k0:n], corner[:], ALU.add).then_inc(a_masked, 1)
                    wait_batch(dve, a_masked, t, 1, 2 * PAIRS, half * PAIRS + i + 1)
                    m = neg_max[:].rearrange("p (h i) -> p h i", i=TT)[:, h:h + 2, j]
                    nc.vector.tensor_reduce(m, pair[:, :, 0:n], AX.X, ALU.max, negate=True).then_inc(a_free, 1)

                def read_y(g):
                    wait_batch(dve, pv_done, t, 0, STEPS, TT * (g + 1))
                    if g == 0:
                        wait_batch(dve, t_full, t, -1, T_UNITS, 1)
                    nc.vector.reciprocal(den_inv[:], den_bank[:]).then_inc(y_inv, 1)
                    wait_batch(dve, y_inv, t, 0, G, g + 1)
                    nc.vector.tensor_tensor(y_norm[:, g, :], y_bank[:], den_inv[:], ALU.mult).then_inc(y_free, 1)

                for s in range(STEPS):
                    if top:
                        for v in units_of(s):
                            max_unit(v)
                    if attend and s and s % TT == 0:
                        read_y(s // TT - 1)
                    if end and s == 1:
                        wait_batch(dve, t_full, t, -1, T_UNITS, 1)
                        wait_batch(dve, x1_loaded, t, -1, DMA, DMA)
                        nc.vector.tensor_tensor(x2[:].rearrange("p i d -> p (i d)"), tail[:],
                                                x1_back[:].rearrange("p i d -> p (i d)"), ALU.add).then_inc(t_free, 1)
                        wait_batch(dve, t_free, t, -1, T_UNITS, 1)
                        moments(x2, t_stats, t_mv, t_dve, 1, 1, -1, t_moments)
                    if end and s == 3:
                        wait_batch(dve, t_rstd_made, t, -1, 1, 1)
                        normalise(xn3, x2, t_mv, t_rstd).then_inc(t_normed, 1)
                    if end and s == 4:
                        wait_batch(dve, t_full, t, -1, T_UNITS, 3)
                        wait_batch(dve, x2b_made, t, -1, 1, 1)
                        wait_batch(dve, out_stored, t, -1, DMA, 0)
                        nc.vector.tensor_tensor(x3[:].rearrange("p i d -> p (i d)"), tail[:],
                                                x2b[:].rearrange("p i d -> p (i d)"), ALU.add).then_inc(t_free, 1)
                    if prep:
                        if s == 0:
                            wait_batch(dve, x_loaded[par], t, 2, *nth(par))
                            moments(x_in[:, par], f_stats[:, 0], f_mv[:, 0], f_dve, 2, 1, 2, f_moments)
                        if s == 1:
                            wait_batch(dve, f_rstd_made, t, 2, 2, 1)
                            wait_batch(dve, f_full, t, 1, F_UNITS, 3)
                            normalise(xn, x_in[:, par], f_mv[:, 0], f_rstd[:, 0]).then_inc(f_normed, 1)
                        if s == 2:
                            wait_batch(dve, f_full, t, 2, F_UNITS, 2)
                            wait_batch(dve, xb_made, t, 2, 1, 1)
                            wait_batch(dve, x1_saved[par], t, 0, *nth(par))
                            nc.vector.tensor_tensor(x1[:, par].rearrange("p i d -> p (i d)"), front[:],
                                                    xb[:].rearrange("p i d -> p (i d)"), ALU.add).then_inc(f_free, 1)
                            wait_batch(dve, f_free, t, 2, F_UNITS, 2)
                            moments(x1[:, par], f_stats[:, 1], f_mv[:, 1], f_dve, 2, 2, 2, f_moments)
                        if s == 4:
                            wait_batch(dve, f_rstd_made, t, 2, 2, 2)
                            normalise(xn, x1[:, par], f_mv[:, 1], f_rstd[:, 1]).then_inc(f_normed, 1)
                        if 5 <= s < 5 + G:
                            g = s - 5
                            wait_batch(dve, qh_made, t, 2, G, g + 1)
                            nc.vector.tensor_tensor(q_low[:, g, :], front[:], q_high[:, g, :].bitcast(F32),
                                                    ALU.subtract).then_inc(f_free, 1)
                        if s == 9:
                            wait_batch(dve, kh_made, t, 2, 1, 1)
                            low = keys_staged[LD:2 * LD, :]
                            nc.vector.tensor_tensor(low, front[LD:2 * LD, :], low.bitcast(F32),
                                                    ALU.subtract).then_inc(f_free, 1)
                if attend:
                    read_y(G - 1)

            rounds(dve, one_round)


_INS = ['L0_attn_x_bld', 'L0_attn_Wq', 'L0_attn_Wkv_down', 'L0_attn_Wk_up', 'L0_attn_Wv_up', 'L0_attn_Wout',
        'L0_ffn_kernel', 'L0_ffn_bias', 'L0_ffn_a', 'L0_ffn_b']
_OUTS = [((16, 512, 128), 'float32')]


def kernel(**inputs):
    import numpy as _np
    import concourse.bacc as _bacc
    from concourse import mybir as _mybir
    from concourse.bass_utils import run_bass_kernel_spmd as _run

    nc = _bacc.Bacc("TRN2", target_bir_lowering=False, num_devices=1)
    arrays, args = {}, []
    for name in _INS:
        a = _np.ascontiguousarray(inputs[name])
        arrays[f"in_{name}_dram"] = a
        args.append(nc.dram_tensor(f"in_{name}_dram", a.shape, _mybir.dt.from_np(a.dtype), kind="ExternalInput").ap())
    for i, (shape, dtype) in enumerate(_OUTS):
        dt = _mybir.dt.from_np(_np.dtype(dtype))
        args.append(nc.dram_tensor(f"out_{i}_dram", shape, dt, kind="ExternalOutput").ap())
    macaron_block(nc, *args)
    r = _run(nc, [arrays], core_ids=[0])
    got = tuple(r.results[0][f"out_{i}_dram"] for i in range(len(_OUTS)))
    return got[0]
```

```python
from contextlib import ExitStack

import concourse.bass as bass
from concourse import mybir

F32 = mybir.dt.float32
F32R = mybir.dt.float32r
ALU = mybir.AluOpType
ACT = mybir.ActivationFunctionType
AX = mybir.AxisListType

P = 128
B, L, D = 16, 512, 128
H, HD, LD = 16, 64, 32
RANK = 16
TT = L // P
HG = P // LD
G = H // HG
EPS = 1e-5
QMAX = 7.0
MASKED = -3.0e38
ROUND = 1.5 * 2.0 ** 23
KS = 3 * LD
KM = KS + 1

F_UNITS = 9
HALF = H // 2
RING = 3
MAX_TILES = HALF * TT
A_DELAY = 6
A_ORDER = ([(0, i) for i in range(MAX_TILES)] + [(1, i) for i in range(A_DELAY)] + [(0, None)]
           + [(1, i) for i in range(A_DELAY, MAX_TILES)] + [(1, None)])
A_UNITS = len(A_ORDER)
A_TURNS = A_UNITS // RING
MAX_T = [A_ORDER.index((half, None)) for half in range(2)]
T_UNITS = 3
STEPS = G * TT
SCORES = STEPS * HG
DMA = 16
Q_DMAS = 3 * HG


def wait_batch(eng, sem, t, off, per, k):
    if isinstance(t, int):
        if t * per + off * per + k > 0:
            eng.wait_ge(sem, t * per + off * per + k)
    else:
        eng.wait_ge(sem, t * per + (off * per + k))


def nth(par):
    return DMA // 2, DMA - DMA // 2 * par


def units_of(s):
    first, n = 2, STEPS - 2
    return [] if s < first else list(range((s - first) * (A_UNITS - 1) // n, (s - first + 1) * (A_UNITS - 1) // n))


FRONT_AT = {1: 0, 2: 1, 4: 2, 5: 3, 6: 4, 7: 5, 8: 6, 9: 7, 10: 8}
TAIL_AT = {3: 0, 5: 1, 6: 2}


def macaron_block(nc, x, wq, wkv_down, wk_up, wv_up, wout, ffn_w, ffn_bias, ffn_a, ffn_b, out):
    ctx = ExitStack()
    with ctx:
        def sb(name, shape, dt=F32):
            return ctx.enter_context(nc.sbuf_tensor(name, shape, dt))

        def sem(name):
            return ctx.enter_context(nc.semaphore(name))

        x_tiles = x.rearrange("b (i p) d -> b p i d", p=P)
        out_tiles = out.rearrange("b (i p) d -> b p i d", p=P)

        wq_in = sb("wq_in", [P, H * HD])
        wk_in = sb("wk_in", [LD, H * HD])
        wv_in = sb("wv_in", [LD, H * HD])
        wout_in = sb("wout_in", [P, H // 2, D])
        wkv3 = sb("wkv3", [P, 3, LD])
        ffn_in = sb("ffn_in", [P, D])
        a_in = sb("a_in", [P, RANK])
        b_in = sb("b_in", [RANK, D])
        half_bias = sb("half_bias", [P, D])
        identity = sb("identity", [P, P])
        ones = sb("ones", [P, P])
        neg_half = sb("neg_half", [P, TT])
        group_ones = sb("group_ones", [P, G, LD])
        corner = sb("corner", [P, L])
        wq_t = sb("wq_t", [P, H // 2, D])
        wk_t = sb("wk_t", [P, H // 2, LD])
        wv_t = sb("wv_t", [P, H // 2, LD])
        a_t = sb("a_t", [RANK, P])
        w_query = sb("w_query", [P, H // 2, 2, LD])
        w_out = sb("w_out", [P, G, D])
        w_ffn = sb("w_ffn", [P, D])
        absmax = sb("absmax", [P, 4])
        quant = sb("quant", [P, 2, D])

        x_in = sb("x_in", [P, 2, TT, D])
        xb = sb("xb", [P, TT, D])
        x1 = sb("x1", [P, 2, TT, D])
        x1_back = sb("x1_back", [P, TT, D])
        x2 = sb("x2", [P, TT, D])
        x2b = sb("x2b", [P, TT, D])
        x3 = sb("x3", [P, TT, D])
        f_stats = sb("f_stats", [P, 2, TT, 6])
        f_mv = sb("f_mv", [P, 2, TT, 2])
        f_var = sb("f_var", [P, 2, TT])
        f_rstd = sb("f_rstd", [P, 2, TT])
        t_stats = sb("t_stats", [P, TT, 6])
        t_mv = sb("t_mv", [P, TT, 2])
        t_var = sb("t_var", [P, TT])
        t_rstd = sb("t_rstd", [P, TT])
        xn = sb("xn", [P, TT, D])
        xn_t = sb("xn_t", [P, L])
        xn3 = sb("xn3", [P, TT, D])
        xn3_t = sb("xn3_t", [P, L])
        q_high = sb("q_high", [P, G, L], F32R)
        q_low = sb("q_low", [P, G, L], F32R)
        lat_staged = sb("lat_staged", [P, TT, LD])
        keys_staged = sb("keys_staged", [KS, L], F32R)
        q_stack = [sb(f"q_stack{i}", [KM, H, L], F32R) for i in range(2)]
        keys = [sb(f"keys{i}", [KM, L], F32R) for i in range(2)]
        lat = [sb(f"lat{i}", [P, TT, LD]) for i in range(2)]
        maxima = sb("maxima", [P, H * TT])
        max_t = [sb(f"max_t{i}", [HALF * TT, P], F32R) for i in range(2)]
        probs = [sb(f"probs{i}", [P, HG, L]) for i in range(2)]
        den = sb("den", [P, L])
        den_inv = sb("den_inv", [P, L])
        den_spread = sb("den_spread", [P, G, L])
        y_sb = sb("y_sb", [P, G, L])

        banks = [ctx.enter_context(nc.psum_tensor(f"bank{i}", [P, L], F32)) for i in range(8)]
        ring, (aux, score0, score1, y_bank, den_bank) = banks[:RING], banks[RING:]
        scores = [score0, score1]

        w_loaded = sem("w_loaded")
        const_made = sem("const_made")
        w_pe = sem("w_pe")
        w_dve = sem("w_dve")
        w_chain = sem("w_chain")
        x_loaded = [sem("x_loaded0"), sem("x_loaded1")]
        xb_made = sem("xb_made")
        f_dve = sem("f_dve")
        f_moments = sem("f_moments")
        f_pool = sem("f_pool")
        f_rstd_made = sem("f_rstd_made")
        f_normed = sem("f_normed")
        f_full = sem("f_full")
        f_free = sem("f_free")
        qh_made = sem("qh_made")
        kh_made = sem("kh_made")
        x1_saved = [sem("x1_saved0"), sem("x1_saved1")]
        x1_loaded = sem("x1_loaded")
        q_stacked = [sem("q_stacked0"), sem("q_stacked1")]
        keys_landed = sem("keys_landed")
        lat_landed = sem("lat_landed")
        a_full = sem("a_full")
        a_free = [sem(f"a_free{i}") for i in range(RING)]
        max_landed = [sem("max_landed0"), sem("max_landed1")]
        s_full = sem("s_full")
        exp_done = sem("exp_done")
        p_ready = sem("p_ready")
        pv_done = sem("pv_done")
        y_free = sem("y_free")
        den_free = sem("den_free")
        den_made = sem("den_made")
        y_normed = sem("y_normed")
        t_dve = sem("t_dve")
        t_moments = sem("t_moments")
        t_pool = sem("t_pool")
        t_rstd_made = sem("t_rstd_made")
        x2b_made = sem("x2b_made")
        t_normed = sem("t_normed")
        t_full = sem("t_full")
        t_free = sem("t_free")
        out_stored = sem("out_stored")
        waits_passed = sem("waits_passed")

        def wait_batch_alone(eng, sem, t, off, per, k):
            wait_batch(eng, sem, t, off, per, k)
            eng.sem_inc(waits_passed, 1)

        def stages(t):
            known = isinstance(t, int)
            return [not known or 0 <= t + off < B for off in (0, 1, 2, -1)]

        LOOP_FROM, LOOP_TO = 2, B - 4

        def rounds(eng, one_round):
            for t in range(-2, LOOP_FROM):
                one_round(t, t % 2)
            with eng.Fori(LOOP_FROM, LOOP_TO, 2) as t:
                one_round(t, 0)
                one_round(t + 1, 1)
            for t in range(LOOP_TO, B + 1):
                one_round(t, t % 2)

        block = ctx.enter_context(nc.Block())

        @block.sync
        def _(sp):
            for dst, src in (
                (wq_in[:], wq.rearrange("d h k -> d (h k)")),
                (wk_in[:], wk_up.rearrange("c h k -> c (h k)")),
                (wv_in[:], wv_up.rearrange("c h k -> c (h k)")),
                (wout_in[:], wout.rearrange("(g e) k o -> (e k) g o", e=2)),
                (ffn_in[:], ffn_w), (a_in[:], ffn_a), (b_in[:], ffn_b),
                (wkv3[:, 0, :], wkv_down), (wkv3[:, 1, :], wkv_down), (wkv3[:, 2, :], wkv_down),
                (half_bias[:], ffn_bias.rearrange("(o f) -> o f", o=1).broadcast_to([P, D])),
            ):
                sp.dma_start(dst, src).then_inc(w_loaded, DMA)
            sp.dma_start(x_in[:, 0], x_tiles[0]).then_inc(x_loaded[0], DMA)

            def one_round(t, par):
                attend, top, prep, end = stages(t)

                def place_max(half):
                    wait_batch_alone(sp, a_free[MAX_T[half] % RING], t, 1 - half, A_TURNS, MAX_T[half] // RING + 1)
                    dst = q_stack[(1 + half + par) % 2][KS:KM, half * HALF:(half + 1) * HALF, :]
                    sp.dma_start(dst.rearrange("o h (i q) -> o (h i) q", q=P).bitcast(F32),
                                 max_t[half][:].bitcast(F32)).then_inc(max_landed[half], DMA)

                if attend:
                    place_max(1)
                if end:
                    wait_batch_alone(sp, x1_saved[1 - par], t, -1, *nth(1 - par))
                    wait_batch_alone(sp, t_free, t, -2, T_UNITS, 1)
                    sp.dma_start(x1_back[:], out_tiles[t - 1]).then_inc(x1_loaded, DMA)
                if not isinstance(t, int) or t + 3 < B:
                    wait_batch_alone(sp, f_normed, t, 1, 2, 1)
                    wait_batch_alone(sp, xb_made, t, 1, 1, 1)
                    sp.dma_start(x_in[:, 1 - par], x_tiles[t + 3]).then_inc(x_loaded[1 - par], DMA)
                if prep:
                    wait_batch_alone(sp, f_free, t, 2, F_UNITS, 2)
                    sp.dma_start(out_tiles[t + 2], x1[:, par]).then_inc(x1_saved[par], DMA)
                if end:
                    wait_batch_alone(sp, t_free, t, -1, T_UNITS, 3)
                    sp.dma_start(out_tiles[t - 1], x3[:]).then_inc(out_stored, DMA)

                def stack_queries(half):
                    wait_batch_alone(sp, f_free, t, 2, F_UNITS, 3 + 2 * (half + 1))
                    wait_batch_alone(sp, s_full, t, 0, SCORES, SCORES // 2 * (half + 1))
                    g0 = 2 * half
                    for e in range(HG):
                        for part, src in enumerate((q_high, q_high, q_low)):
                            dst = q_stack[par][part * LD:(part + 1) * LD, g0 * HG:(g0 + 2) * HG, :]
                            dst = dst.rearrange("c (g e) l -> c g e l", e=HG)[:, :, e, :]
                            sp.dma_start(dst.bitcast(F32), src[e * LD:(e + 1) * LD, g0:g0 + 2, :].bitcast(F32)).then_inc(q_stacked[half], DMA)

                if prep:
                    stack_queries(0)
                if top:
                    place_max(0)
                if prep:
                    wait_batch_alone(sp, f_free, t, 2, F_UNITS, 8)
                    wait_batch_alone(sp, s_full, t, 0, SCORES, SCORES)
                    sp.dma_start(keys[par][0:KS, :].bitcast(F32), keys_staged[:].bitcast(F32)).then_inc(keys_landed, DMA)
                    stack_queries(1)
                    wait_batch_alone(sp, f_free, t, 2, F_UNITS, 9)
                    wait_batch_alone(sp, pv_done, t, 0, STEPS, STEPS)
                    sp.dma_start(lat[par][:], lat_staged[:]).then_inc(lat_landed, DMA)

            rounds(sp, one_round)
            sp.wait_ge(out_stored, DMA * B)
            for saved in x1_saved:
                sp.wait_ge(saved, DMA * B // 2)

        @block.gpsimd
        def _(pool):
            nc.gpsimd.memset(identity[:], 0.0).then_inc(const_made, 1)
            nc.gpsimd.memset(ones[:], 1.0).then_inc(const_made, 1)
            nc.gpsimd.memset(neg_half[:], -0.5).then_inc(const_made, 1)
            nc.gpsimd.memset(corner[:], 0.0).then_inc(const_made, 1)
            nc.gpsimd.memset(group_ones[:], 0.0).then_inc(const_made, 1)
            pool.wait_ge(const_made, 7)
            nc.gpsimd.affine_select(out=identity[:], in_=identity[:], compare_op=ALU.not_equal, fill=1.0, base=0,
                                    pattern=[[-1, P]], channel_multiplier=1).then_inc(const_made, 1)
            nc.gpsimd.affine_select(out=corner[:, L - P:], in_=corner[:, L - P:], compare_op=ALU.is_ge, fill=MASKED, base=0,
                                    pattern=[[-1, P]], channel_multiplier=1).then_inc(const_made, 1)
            for g in range(G):
                nc.gpsimd.memset(group_ones[:, g, g::G], 1.0).then_inc(const_made, 1)
                pool.wait_ge(const_made, 10 + g)
            pool.wait_ge(w_dve, 1)

            def one_round(t, par):
                attend, top, prep, end = stages(t)

                def rstd(moments, per, k, off, mv, var, out_, chain, done):
                    wait_batch_alone(pool, moments, t, off, per, k)
                    nc.gpsimd.tensor_scalar(var, mv, EPS, None, ALU.add).then_inc(chain, 1)
                    wait_batch(pool, chain, t, off, per, k)
                    nc.gpsimd.tensor_tensor(out_, var, neg_half[:], ALU.pow).then_inc(done, 1)

                for s in range(STEPS):
                    if prep and s == 0:
                        wait_batch(pool, x_loaded[par], t, 2, *nth(par))
                        wait_batch(pool, f_free, t, 1, F_UNITS, 2)
                        nc.gpsimd.tensor_tensor(xb[:], x_in[:, par], half_bias[:, None, :].broadcast_to([P, TT, D]),
                                                ALU.add).then_inc(xb_made, 1)
                        rstd(f_moments, 2, 1, 2, f_mv[:, 0, :, 1], f_var[:, 0], f_rstd[:, 0], f_pool, f_rstd_made)
                    if attend:
                        n = min(P, L)
                        wait_batch_alone(pool, exp_done, t, 0, SCORES, HG * (s + 1))
                        diag = probs[s % 2][:, :, 0:n]
                        nc.gpsimd.affine_select(out=diag, in_=diag, compare_op=ALU.is_ge, fill=0.0, base=0,
                                                pattern=[[0, HG], [1, n]], channel_multiplier=-1).then_inc(p_ready, 1)
                    if end and s == 3:
                        rstd(t_moments, 1, 1, -1, t_mv[:, :, 1], t_var[:], t_rstd[:], t_pool, t_rstd_made)
                    if prep and s == 2:
                        rstd(f_moments, 2, 2, 2, f_mv[:, 1, :, 1], f_var[:, 1], f_rstd[:, 1], f_pool, f_rstd_made)
                    if end and s == 4:
                        wait_batch(pool, t_free, t, -1, T_UNITS, 1)
                        nc.gpsimd.tensor_tensor(x2b[:], x2[:], half_bias[:, None, :].broadcast_to([P, TT, D]),
                                                ALU.add).then_inc(x2b_made, 1)

            rounds(pool, one_round)

        @block.scalar
        def _(act):
            def one_round(t, par):
                attend, top, prep, end = stages(t)

                def read_max(half):
                    v = MAX_T[half]
                    wait_batch(act, a_full, t, 1 - half, A_UNITS, v + 1)
                    wait_batch(act, max_landed[half], t, 1 - half, DMA, 0)
                    nc.scalar.activation(max_t[half][:], ring[v % RING][0:MAX_TILES, 0:P], ACT.Copy,
                                         scale=-1.0).then_inc(a_free[v % RING], 1)

                def exp(s, e):
                    n = L - P * (s % TT)
                    u = HG * s + e
                    wait_batch(act, s_full, t, 0, SCORES, u + 1)
                    if e == 0:
                        wait_batch(act, pv_done, t, 0, STEPS, s - 1)
                    nc.scalar.activation(probs[s % 2][:, e, 0:n], scores[u % 2][:, 0:n], ACT.Exp).then_inc(exp_done, 1)

                def read_y(g):
                    wait_batch(act, pv_done, t, 0, STEPS, TT * (g + 1))
                    if g == 0:
                        wait_batch(act, t_full, t, -1, T_UNITS, 1)
                    nc.scalar.activation(y_sb[:, g, :], y_bank[:], ACT.Copy).then_inc(y_free, 1)

                if attend:
                    read_max(1)
                for s in range(STEPS):
                    if attend:
                        exp(s, 0)
                        exp(s, 1)
                    if top and MAX_T[0] in units_of(s):
                        read_max(0)
                    if attend:
                        exp(s, 2)
                        exp(s, 3)
                        if s and s % TT == 0:
                            read_y(s // TT - 1)
                    if end and s == 5:
                        wait_batch(act, t_full, t, -1, T_UNITS, 2)
                        nc.scalar.activation(xn3_t[:], aux[:], ACT.Copy).then_inc(t_free, 1)
                    if prep:
                        if s in (1, 4):
                            wait_batch(act, f_full, t, 2, F_UNITS, 1 if s == 1 else 3)
                            nc.scalar.activation(xn_t[:], aux[:], ACT.Copy).then_inc(f_free, 1)
                        if 5 <= s < 5 + G:
                            g = s - 5
                            wait_batch(act, f_full, t, 2, F_UNITS, 4 + g)
                            wait_batch(act, q_stacked[g // 2], t, 2, Q_DMAS * DMA, 0)
                            nc.scalar.activation(q_high[:, g, :], aux[:], ACT.Copy).then_inc(qh_made, 1)
                        if s == 9:
                            wait_batch(act, f_full, t, 2, F_UNITS, 8)
                            wait_batch(act, keys_landed, t, 2, DMA, 0)
                            nc.scalar.activation(keys_staged[:], aux[0:KS, :], ACT.Copy).then_inc(kh_made, 1)
                        if s == 10:
                            wait_batch(act, f_full, t, 2, F_UNITS, 9)
                            wait_batch(act, lat_landed, t, 2, DMA, 0)
                            nc.scalar.activation(lat_staged[:].rearrange("p i c -> p (i c)"), aux[:, 0:TT * LD],
                                                 ACT.Copy).then_inc(f_free, 1)
                if attend:
                    read_y(G - 1)
                    nc.scalar.activation(den[:], den_bank[:], ACT.Copy).then_inc(den_free, 1)

            rounds(act, one_round)

        @block.tensor
        def _(pe):
            pe.wait_ge(w_loaded, 11 * DMA)
            pe.wait_ge(const_made, 9 + G)
            for j in range(H // 2):
                nc.tensor.transpose(ring[j // 4][:, (j % 4) * P:(j % 4 + 1) * P], wq_in[:, j * P:(j + 1) * P], identity[:])
                nc.tensor.transpose(ring[2][:, j * LD:(j + 1) * LD], wk_in[:, j * P:(j + 1) * P], identity[0:LD, 0:LD])
                nc.tensor.transpose(aux[:, j * LD:(j + 1) * LD], wv_in[:, j * P:(j + 1) * P], identity[0:LD, 0:LD])
            nc.tensor.transpose(score0[0:RANK, 0:P], a_in[:], identity[:]).then_inc(w_pe, 1)
            pe.wait_ge(w_dve, 2)
            nc.tensor.transpose(score1[0:1, 0:P], absmax[:, 0:1], identity[:]).then_inc(w_pe, 1)
            nc.tensor.matmul(score0[:, 0:D], a_t[:], b_in[:], start=True, stop=True)
            for odd, (q_bank, o_bank) in enumerate(((ring[2], y_bank), (aux, den_bank))):
                rows = slice(odd * HD, (odd + 1) * HD)
                for j in range(H // 2):
                    e, g = (2 * j + odd) % HG, (2 * j + odd) // HG
                    nc.tensor.matmul(q_bank[:, j * LD:(j + 1) * LD], wq_t[rows, j, :], wk_t[rows, j, :],
                                     start=True, stop=True)
                    last = nc.tensor.matmul(o_bank[e * LD:(e + 1) * LD, g * D:(g + 1) * D], wv_t[rows, j, :],
                                            wout_in[rows, j, :], start=True, stop=True)
            last.then_inc(w_pe, 1)
            pe.wait_ge(w_dve, 3)
            nc.tensor.matmul(score1[:, 0:1], ones[0:1, :], absmax[0:1, 2:3], start=True, stop=True).then_inc(w_pe, 1)
            pe.wait_ge(w_dve, 4)

            def one_round(t, par):
                attend, top, prep, end = stages(t)

                def score(s, e):
                    g, j = divmod(s, TT)
                    u = HG * s + e
                    if e == 0 and j == 0 and g % 2 == 0:
                        wait_batch(pe, max_landed[g // 2], t, 0, DMA, DMA)
                    wait_batch(pe, exp_done, t, 0, SCORES, u - 1)
                    nc.tensor.matmul(scores[u % 2][:, 0:L - P * j], keys[par][:, j * P:(j + 1) * P],
                                     q_stack[par][:, g * HG + e, j * P:L], start=True, stop=True).then_inc(s_full, 1)

                def weigh_latents(s):
                    g, j = divmod(s, TT)
                    wait_batch(pe, p_ready, t, 0, STEPS, s + 1)
                    if s == 0:
                        wait_batch(pe, lat_landed, t, 0, DMA, DMA)
                    if j == 0:
                        wait_batch(pe, y_free, t, 0, G, g)
                    for e in range(HG):
                        nc.tensor.matmul(y_bank[e * LD:(e + 1) * LD, j * P:L], lat[par][:, j, :],
                                         probs[s % 2][:, e, 0:L - P * j], start=(j == 0), stop=(j == TT - 1))

                def weigh_ones(s):
                    g, j = divmod(s, TT)
                    if s == 0:
                        wait_batch(pe, den_free, t, 0, 1, 0)
                    for e in range(HG):
                        last = nc.tensor.matmul(den_bank[e * LD:(e + 1) * LD, j * P:L], group_ones[:, g, :],
                                                probs[s % 2][:, e, 0:L - P * j], start=(s == 0), stop=(s == STEPS - 1))
                    last.then_inc(pv_done, 1)

                def max_unit(v):
                    half, i = A_ORDER[v]
                    off, bank = 1, ring[v % RING]
                    if v == MAX_T[1]:
                        off = 0
                    wait_batch(pe, a_free[v % RING], t, off, A_TURNS, v // RING)
                    if i is None:
                        for w in (v - 1, v - 2):
                            wait_batch(pe, a_free[w % RING], t, off, A_TURNS, w // RING + 1)
                        nc.tensor.transpose(bank[0:MAX_TILES, 0:P], maxima[:, half * MAX_TILES:(half + 1) * MAX_TILES],
                                            identity[:]).then_inc(a_full, 1)
                        return
                    if i == 0:
                        wait_batch(pe, q_stacked[half], t, 1, Q_DMAS * DMA, Q_DMAS * DMA)
                        if half == 0:
                            wait_batch(pe, keys_landed, t, 1, DMA, DMA)
                    h, j = half * HALF + i // TT, i % TT
                    nc.tensor.matmul(bank[:, 0:P * (j + 1)], q_stack[1 - par][0:KS, h, j * P:(j + 1) * P],
                                     keys[1 - par][0:KS, 0:P * (j + 1)], start=True, stop=True).then_inc(a_full, 1)

                def front_unit(u):
                    wait_batch(pe, f_free, t, 2, F_UNITS, u)
                    if end and u in (2, 3, 4):
                        wait_batch(pe, t_free, t, -1, T_UNITS, u - 1)
                    if u in (0, 2):
                        wait_batch(pe, f_normed, t, 2, 2, 1 + u // 2)
                        for i in range(TT):
                            last = nc.tensor.transpose(aux[:, i * P:(i + 1) * P], xn[:, i, :], identity[:])
                    elif u == 1:
                        for i in range(TT):
                            last = nc.tensor.matmul(aux[:, i * D:(i + 1) * D], xn_t[:, i * P:(i + 1) * P], w_ffn[:],
                                                    start=True, stop=True)
                    elif u < 7:
                        w = w_query[:, 2 * (u - 3):2 * (u - 2)].rearrange("p j e c -> p (j e c)")
                        last = nc.tensor.matmul(aux[:], w, xn_t[:], start=True, stop=True)
                    elif u == 7:
                        last = nc.tensor.matmul(aux[0:KS, :], wkv3[:].rearrange("p r c -> p (r c)"), xn_t[:],
                                                start=True, stop=True)
                    else:
                        for i in range(TT):
                            last = nc.tensor.matmul(aux[:, i * LD:(i + 1) * LD], xn_t[:, i * P:(i + 1) * P],
                                                    wkv3[:, 0, :], start=True, stop=True)
                    last.then_inc(f_full, 1)

                def tail_unit(u):
                    wait_batch(pe, t_free, t, -1, T_UNITS, u)
                    if prep:
                        wait_batch(pe, f_free, t, 2, F_UNITS, u + 2)
                    elif u == 0:
                        pe.wait_ge(f_free, F_UNITS * B)
                    if u == 0:
                        wait_batch(pe, y_normed, t, -1, 1, 1)
                        for i in range(TT):
                            for g in range(G):
                                last = nc.tensor.matmul(aux[:, i * D:(i + 1) * D], y_sb[:, g, i * P:(i + 1) * P],
                                                        w_out[:, g, :], start=(g == 0), stop=(g == G - 1))
                    elif u == 1:
                        wait_batch(pe, t_normed, t, -1, 1, 1)
                        for i in range(TT):
                            last = nc.tensor.transpose(aux[:, i * P:(i + 1) * P], xn3[:, i, :], identity[:])
                    else:
                        for i in range(TT):
                            last = nc.tensor.matmul(aux[:, i * D:(i + 1) * D], xn3_t[:, i * P:(i + 1) * P], w_ffn[:],
                                                    start=True, stop=True)
                    last.then_inc(t_full, 1)

                if attend:
                    max_unit(MAX_T[1])
                for s in range(STEPS):
                    tiles = units_of(s) if top else []
                    if attend:
                        score(s, 0)
                        score(s, 1)
                    for v in tiles[:2]:
                        max_unit(v)
                    if attend:
                        score(s, 2)
                        if s:
                            weigh_latents(s - 1)
                    for v in tiles[2:4]:
                        max_unit(v)
                    if attend:
                        score(s, 3)
                        if s:
                            weigh_ones(s - 1)
                    for v in tiles[4:]:
                        max_unit(v)
                    if end and s in TAIL_AT:
                        tail_unit(TAIL_AT[s])
                    if prep and s in FRONT_AT:
                        front_unit(FRONT_AT[s])
                if attend:
                    weigh_latents(STEPS - 1)
                    weigh_ones(STEPS - 1)

            rounds(pe, one_round)

        @block.vector
        def _(dve):
            nc.vector.memset(keys[0][KS:KM, :].bitcast(F32), 1.0).then_inc(const_made, 1)
            nc.vector.memset(keys[1][KS:KM, :].bitcast(F32), 1.0).then_inc(const_made, 1)
            dve.wait_ge(w_loaded, 11 * DMA)
            nc.vector.tensor_scalar(half_bias[:], half_bias[:], 0.5, None, ALU.mult).then_inc(w_dve, 1)
            nc.vector.tensor_reduce(absmax[:, 0:1], ffn_in[:], AX.X, ALU.max, apply_absolute_value=True)
            dve.wait_ge(w_pe, 1)
            for i in range(2):
                nc.vector.tensor_copy(wq_t[:, i * 4:(i + 1) * 4, :].rearrange("p j d -> p (j d)"), ring[i][:])
            nc.vector.tensor_copy(wk_t[:].rearrange("p j c -> p (j c)"), ring[2][:, 0:H // 2 * LD])
            nc.vector.tensor_copy(wv_t[:].rearrange("p j c -> p (j c)"), aux[:, 0:H // 2 * LD])
            nc.vector.tensor_copy(a_t[:], score0[0:RANK, 0:P]).then_inc(w_dve, 1)
            dve.wait_ge(w_pe, 2)
            chain = [0]

            def link(ins):
                chain[0] += 1
                ins.then_inc(w_chain, 1)
                dve.wait_ge(w_chain, chain[0])

            link(nc.vector.tensor_reduce(absmax[0:1, 1:2], score1[0:1, 0:P], AX.X, ALU.max))
            nc.vector.tensor_scalar(absmax[0:1, 2:3], absmax[0:1, 1:2], 1.0 / QMAX, None, ALU.mult).then_inc(w_dve, 1)
            dve.wait_ge(w_pe, 3)
            for odd, (q_bank, o_bank) in enumerate(((ring[2], y_bank), (aux, den_bank))):
                nc.vector.tensor_scalar(w_query[:, :, odd, :], q_bank[:, 0:H // 2 * LD].rearrange("p (j c) -> p j c", c=LD),
                                        HD ** -0.5, None, ALU.mult)
                for e in (odd, odd + 2):
                    rows = slice(e * LD, (e + 1) * LD)
                    nc.vector.tensor_copy(w_out[rows].rearrange("p g o -> p (g o)"), o_bank[rows, :])
            dve.wait_ge(w_pe, 4)
            link(nc.vector.tensor_copy(absmax[:, 3:4], score1[:, 0:1]))
            link(nc.vector.reciprocal(absmax[:, 1:2], absmax[:, 3:4]))
            link(nc.vector.tensor_scalar(quant[:, 0], ffn_in[:], absmax[:, 1:2], ROUND, ALU.mult, ALU.add))
            link(nc.vector.tensor_scalar(quant[:, 1], quant[:, 0], -ROUND, QMAX, ALU.add, ALU.min))
            link(nc.vector.tensor_scalar(quant[:, 0], quant[:, 1], -QMAX - 1.0, absmax[:, 3:4], ALU.max, ALU.mult))
            link(nc.vector.tensor_tensor(quant[:, 1], score0[:, 0:D], quant[:, 0], ALU.add))
            nc.vector.tensor_scalar(w_ffn[:], quant[:, 1], 0.5, None, ALU.mult).then_inc(w_dve, 1)

            def one_round(t, par):
                attend, top, prep, end = stages(t)

                def moments(src, stats, mv, chain, per, k, off, done):
                    for i in range(TT):
                        last = nc.vector.bn_stats(stats[:, i, :], src[:, i, :])
                    last.then_inc(chain, 1)
                    wait_batch_alone(dve, chain, t, off, per, k)
                    for i in range(TT):
                        last = nc.vector.bn_aggr(mv[:, i, :], stats[:, i, :])
                    last.then_inc(done, 1)

                def normalise(dst, src, mv, rstd):
                    for i in range(TT):
                        last = nc.vector.tensor_scalar(dst[:, i, :], src[:, i, :], mv[:, i, 0:1], rstd[:, i:i + 1],
                                                       ALU.subtract, ALU.mult)
                    return last

                def max_unit(v):
                    half, i = A_ORDER[v]
                    if i is None:
                        return
                    h, j = half * HALF + i // TT, i % TT
                    n = P * (j + 1)
                    wait_batch_alone(dve, a_full, t, 1, A_UNITS, v + 1)
                    bank = ring[v % RING][:, 0:n]
                    nc.vector.tensor_tensor_reduce(out=bank, in0=bank, in1=corner[:, L - n:],
                                                   scale=1.0, scalar=MASKED, op0=ALU.add, op1=ALU.max,
                                                   accum_out=maxima[:, h * TT + j:h * TT + j + 1]).then_inc(a_free[v % RING], 1)

                def normalise_y():
                    wait_batch(dve, den_free, t, -1, 1, 1)
                    nc.vector.reciprocal(den_inv[:], den[:]).then_inc(den_made, 1)
                    wait_batch_alone(dve, den_made, t, -1, 2, 1)
                    for g in range(G):
                        last = nc.vector.stream_shuffle(den_spread[:, g, :], den_inv[:], [g] * LD)
                    last.then_inc(den_made, 1)
                    wait_batch(dve, den_made, t, -1, 2, 2)
                    nc.vector.tensor_tensor(y_sb[:], y_sb[:], den_spread[:], ALU.mult).then_inc(y_normed, 1)

                for s in range(STEPS):
                    if top:
                        for v in units_of(s):
                            max_unit(v)
                    if end and s == 0:
                        normalise_y()
                    if end and s == 3:
                        wait_batch(dve, t_full, t, -1, T_UNITS, 1)
                        wait_batch(dve, x1_loaded, t, -1, DMA, DMA)
                        nc.vector.tensor_tensor(x2[:].rearrange("p i d -> p (i d)"), aux[:],
                                                x1_back[:].rearrange("p i d -> p (i d)"), ALU.add).then_inc(t_free, 1)
                        wait_batch(dve, t_free, t, -1, T_UNITS, 1)
                        moments(x2, t_stats, t_mv, t_dve, 1, 1, -1, t_moments)
                    if end and s == 5:
                        wait_batch(dve, t_rstd_made, t, -1, 1, 1)
                        normalise(xn3, x2, t_mv, t_rstd).then_inc(t_normed, 1)
                    if end and s == 6:
                        wait_batch(dve, t_full, t, -1, T_UNITS, 3)
                        wait_batch(dve, x2b_made, t, -1, 1, 1)
                        wait_batch(dve, out_stored, t, -1, DMA, 0)
                        nc.vector.tensor_tensor(x3[:].rearrange("p i d -> p (i d)"), aux[:],
                                                x2b[:].rearrange("p i d -> p (i d)"), ALU.add).then_inc(t_free, 1)
                    if prep:
                        if s == 0:
                            wait_batch(dve, x_loaded[par], t, 2, *nth(par))
                            moments(x_in[:, par], f_stats[:, 0], f_mv[:, 0], f_dve, 2, 1, 2, f_moments)
                        if s == 1:
                            wait_batch(dve, f_rstd_made, t, 2, 2, 1)
                            wait_batch(dve, f_full, t, 1, F_UNITS, 3)
                            normalise(xn, x_in[:, par], f_mv[:, 0], f_rstd[:, 0]).then_inc(f_normed, 1)
                        if s == 2:
                            wait_batch(dve, f_full, t, 2, F_UNITS, 2)
                            wait_batch(dve, xb_made, t, 2, 1, 1)
                            wait_batch(dve, x1_saved[par], t, 0, *nth(par))
                            nc.vector.tensor_tensor(x1[:, par].rearrange("p i d -> p (i d)"), aux[:],
                                                    xb[:].rearrange("p i d -> p (i d)"), ALU.add).then_inc(f_free, 1)
                            wait_batch(dve, f_free, t, 2, F_UNITS, 2)
                            moments(x1[:, par], f_stats[:, 1], f_mv[:, 1], f_dve, 2, 2, 2, f_moments)
                        if s == 4:
                            wait_batch(dve, f_rstd_made, t, 2, 2, 2)
                            normalise(xn, x1[:, par], f_mv[:, 1], f_rstd[:, 1]).then_inc(f_normed, 1)
                        if 5 <= s < 5 + G:
                            g = s - 5
                            wait_batch(dve, qh_made, t, 2, G, g + 1)
                            nc.vector.tensor_tensor(q_low[:, g, :], aux[:], q_high[:, g, :].bitcast(F32),
                                                    ALU.subtract).then_inc(f_free, 1)
                        if s == 9:
                            wait_batch(dve, kh_made, t, 2, 1, 1)
                            low = keys_staged[LD:2 * LD, :]
                            nc.vector.tensor_tensor(low, aux[LD:2 * LD, :], low.bitcast(F32),
                                                    ALU.subtract).then_inc(f_free, 1)
            rounds(dve, one_round)


_INS = ['L0_attn_x_bld', 'L0_attn_Wq', 'L0_attn_Wkv_down', 'L0_attn_Wk_up', 'L0_attn_Wv_up', 'L0_attn_Wout',
        'L0_ffn_kernel', 'L0_ffn_bias', 'L0_ffn_a', 'L0_ffn_b']
_OUTS = [((16, 512, 128), 'float32')]


def kernel(**inputs):
    import numpy as _np
    import concourse.bacc as _bacc
    from concourse import mybir as _mybir
    from concourse.bass_utils import run_bass_kernel_spmd as _run

    nc = _bacc.Bacc("TRN2", target_bir_lowering=False, num_devices=1)
    arrays, args = {}, []
    for name in _INS:
        a = _np.ascontiguousarray(inputs[name])
        arrays[f"in_{name}_dram"] = a
        args.append(nc.dram_tensor(f"in_{name}_dram", a.shape, _mybir.dt.from_np(a.dtype), kind="ExternalInput").ap())
    for i, (shape, dtype) in enumerate(_OUTS):
        dt = _mybir.dt.from_np(_np.dtype(dtype))
        args.append(nc.dram_tensor(f"out_{i}_dram", shape, dt, kind="ExternalOutput").ap())
    macaron_block(nc, *args)
    r = _run(nc, [arrays], core_ids=[0])
    got = tuple(r.results[0][f"out_{i}_dram"] for i in range(len(_OUTS)))
    return got[0]
```

```python
from contextlib import ExitStack

import concourse.bass as bass
from concourse import mybir

F32 = mybir.dt.float32
F32R = mybir.dt.float32r
ALU = mybir.AluOpType
ACT = mybir.ActivationFunctionType
AX = mybir.AxisListType

P = 128
B, L, D = 16, 512, 128
H, HD, LD = 16, 64, 32
RANK = 16
TT = L // P
HG = P // LD
G = H // HG
EPS = 1e-5
QMAX = 7.0
MASKED = -3.0e38
ROUND = 1.5 * 2.0 ** 23
KS = 3 * LD
KM = KS + 1

F_UNITS = 9
HALF = H // 2
RING = 3
MAX_TILES = HALF * TT
A_DELAY = 6
A_ORDER = ([(0, i) for i in range(MAX_TILES)] + [(1, i) for i in range(A_DELAY)] + [(0, None)]
           + [(1, i) for i in range(A_DELAY, MAX_TILES)] + [(1, None)])
A_UNITS = len(A_ORDER)
A_TURNS = A_UNITS // RING
MAX_T = [A_ORDER.index((half, None)) for half in range(2)]
T_UNITS = 3
STEPS = G * TT
SHARED = [L // (L - P * j) for j in range(TT)]
SHARED = [n - n % 2 if n > 1 else 1 for n in SHARED]
GROUP_SCORES = sum(HG // n for n in SHARED)
SCORES = G * GROUP_SCORES
DMA = 16
Q_DMAS = 3 * HG


def wait_batch(eng, sem, t, off, per, k):
    if isinstance(t, int):
        if t * per + off * per + k > 0:
            eng.wait_ge(sem, t * per + off * per + k)
    else:
        eng.wait_ge(sem, t * per + (off * per + k))


def nth(par):
    return DMA // 2, DMA - DMA // 2 * par


A_SHARE = [0, 4, 3, 2, 2, 3, 6, 7, 4, 5, 5, 6, 5, 4, 5, 4]
assert sum(A_SHARE) == A_UNITS - 1 and len(A_SHARE) == STEPS


def units_of(s):
    first = sum(A_SHARE[:s])
    return list(range(first, first + A_SHARE[s]))


def score_unit(s, e):
    g, j = divmod(s, TT)
    return g * GROUP_SCORES + sum(HG // n for n in SHARED[:j]) + e // SHARED[j]


FRONT_AT = [1, 2, 5, 6, 8, 9, 11, 13, 14]
TAIL_AT = [7, 10, 12]
LAG = 2
BUFS = 4


def macaron_block(nc, x, wq, wkv_down, wk_up, wv_up, wout, ffn_w, ffn_bias, ffn_a, ffn_b, out):
    ctx = ExitStack()
    with ctx:
        def sb(name, shape, dt=F32):
            return ctx.enter_context(nc.sbuf_tensor(name, shape, dt))

        def sem(name):
            return ctx.enter_context(nc.semaphore(name))

        x_tiles = x.rearrange("b (i p) d -> b p i d", p=P)
        out_tiles = out.rearrange("b (i p) d -> b p i d", p=P)

        wq_in = sb("wq_in", [P, H * HD])
        wk_in = sb("wk_in", [LD, H * HD])
        wv_in = sb("wv_in", [LD, H * HD])
        wout_in = sb("wout_in", [P, H // 2, D])
        wkv3 = sb("wkv3", [P, 3, LD])
        ffn_in = sb("ffn_in", [P, D])
        a_in = sb("a_in", [P, RANK])
        b_in = sb("b_in", [RANK, D])
        half_bias = sb("half_bias", [P, D])
        identity = sb("identity", [P, P])
        ones = sb("ones", [P, P])
        neg_half = sb("neg_half", [P, TT])
        group_ones = sb("group_ones", [P, G, LD])
        corner = sb("corner", [P, L])
        wq_t = sb("wq_t", [P, H // 2, D])
        wk_t = sb("wk_t", [P, H // 2, LD])
        wv_t = sb("wv_t", [P, H // 2, LD])
        a_t = sb("a_t", [RANK, P])
        w_query = sb("w_query", [P, H // 2, 2, LD])
        w_out = sb("w_out", [P, G, D])
        w_ffn = sb("w_ffn", [P, D])
        absmax = sb("absmax", [P, 4])
        quant = sb("quant", [P, 2, D])

        x_in = sb("x_in", [P, 2, TT, D])
        xb = sb("xb", [P, TT, D])
        x1 = sb("x1", [P, 2, TT, D])
        x1_back = sb("x1_back", [P, TT, D])
        x2 = sb("x2", [P, TT, D])
        x2b = sb("x2b", [P, TT, D])
        x3 = sb("x3", [P, TT, D])
        f_stats = sb("f_stats", [P, 2, TT, 6])
        f_mv = sb("f_mv", [P, 2, TT, 2])
        f_var = sb("f_var", [P, 2, TT])
        f_rstd = sb("f_rstd", [P, 2, TT])
        f_shift = sb("f_shift", [P, 2, TT])
        t_stats = sb("t_stats", [P, TT, 6])
        t_mv = sb("t_mv", [P, TT, 2])
        t_var = sb("t_var", [P, TT])
        t_rstd = sb("t_rstd", [P, TT])
        t_shift = sb("t_shift", [P, 2, TT])
        xn = sb("xn", [P, TT, D])
        xn_t = sb("xn_t", [P, L])
        xn3 = sb("xn3", [P, TT, D])
        xn3_t = sb("xn3_t", [P, L])
        q_high = sb("q_high", [P, G, L], F32R)
        q_low = sb("q_low", [P, G, L], F32R)
        lat_staged = sb("lat_staged", [P, TT, LD])
        keys_staged = sb("keys_staged", [KS, L], F32R)
        q_stack = [sb(f"q_stack{i}", [KM, H, L], F32R) for i in range(2)]
        keys = [sb(f"keys{i}", [KM, L], F32R) for i in range(2)]
        lat = [sb(f"lat{i}", [P, TT, LD]) for i in range(2)]
        maxima = sb("maxima", [P, H * TT])
        max_t = [sb(f"max_t{i}", [HALF * TT, P], F32R) for i in range(2)]
        probs = [sb(f"probs{i}", [P, HG, L]) for i in range(BUFS)]
        den = sb("den", [P, L])
        den_inv = sb("den_inv", [P, L])
        y_sb = sb("y_sb", [P, G, L])
        y_norm = sb("y_norm", [P, G, L])

        banks = [ctx.enter_context(nc.psum_tensor(f"bank{i}", [P, L], F32)) for i in range(8)]
        ring, (aux, score0, score1, y_bank, den_bank) = banks[:RING], banks[RING:]
        scores = [score0, score1]

        ffn_loaded = sem("ffn_loaded")
        w_loaded = sem("w_loaded")
        const_made = sem("const_made")
        w_pe = sem("w_pe")
        w_dve = sem("w_dve")
        w_chain = sem("w_chain")
        x_loaded = [sem("x_loaded0"), sem("x_loaded1")]
        xb_made = sem("xb_made")
        f_dve = sem("f_dve")
        f_moments = sem("f_moments")
        f_pool = sem("f_pool")
        f_rstd_made = sem("f_rstd_made")
        f_normed = sem("f_normed")
        f_full = sem("f_full")
        f_free = sem("f_free")
        qh_made = sem("qh_made")
        kh_made = sem("kh_made")
        x1_saved = [sem("x1_saved0"), sem("x1_saved1")]
        x1_loaded = sem("x1_loaded")
        q_stacked = [sem("q_stacked0"), sem("q_stacked1")]
        keys_landed = sem("keys_landed")
        lat_landed = sem("lat_landed")
        a_full = sem("a_full")
        a_free = [sem(f"a_free{i}") for i in range(RING)]
        max_landed = [sem("max_landed0"), sem("max_landed1")]
        s_full = sem("s_full")
        exp_done = sem("exp_done")
        p_ready = sem("p_ready")
        pv_done = sem("pv_done")
        y_full = sem("y_full")
        y_free = sem("y_free")
        den_free = sem("den_free")
        den_made = sem("den_made")
        y_normed = sem("y_normed")
        t_dve = sem("t_dve")
        t_moments = sem("t_moments")
        t_pool = sem("t_pool")
        t_rstd_made = sem("t_rstd_made")
        x2b_made = sem("x2b_made")
        t_normed = sem("t_normed")
        t_full = sem("t_full")
        t_free = sem("t_free")
        out_stored = sem("out_stored")
        waits_passed = sem("waits_passed")

        def wait_batch_alone(eng, sem, t, off, per, k):
            wait_batch(eng, sem, t, off, per, k)
            eng.sem_inc(waits_passed, 1)

        def stages(t):
            known = isinstance(t, int)
            return [not known or 0 <= t + off < B for off in (0, 1, 2, -1)]

        def is_first(t):
            return isinstance(t, int) and t == -2

        def front_bank(t, u):
            own = (score0, score1, y_bank, den_bank)
            return own[u - 3] if is_first(t) and 3 <= u < 3 + G else aux

        LOOP_FROM, LOOP_TO = 2, B - 4

        def rounds(eng, one_round):
            for t in range(-2, LOOP_FROM):
                one_round(t, t % 2)
            with eng.Fori(LOOP_FROM, LOOP_TO, 2) as t:
                one_round(t, 0)
                one_round(t + 1, 1)
            for t in range(LOOP_TO, B + 1):
                one_round(t, t % 2)

        block = ctx.enter_context(nc.Block())

        @block.sync
        def _(sp):
            sp.dma_start(x_in[:, 0], x_tiles[0]).then_inc(x_loaded[0], DMA)
            for dst, src in (
                (ffn_in[:], ffn_w), (a_in[:], ffn_a), (b_in[:], ffn_b),
                (half_bias[:], ffn_bias.rearrange("(o f) -> o f", o=1).broadcast_to([P, D])),
            ):
                sp.dma_start(dst, src).then_inc(ffn_loaded, DMA)
            for dst, src in (
                (wq_in[:], wq.rearrange("d h k -> d (h k)")),
                (wk_in[:], wk_up.rearrange("c h k -> c (h k)")),
                (wv_in[:], wv_up.rearrange("c h k -> c (h k)")),
                (wout_in[:], wout.rearrange("(g e) k o -> (e k) g o", e=2)),
                (wkv3[:, 0, :], wkv_down), (wkv3[:, 1, :], wkv_down), (wkv3[:, 2, :], wkv_down),
            ):
                sp.dma_start(dst, src).then_inc(w_loaded, DMA)

            def one_round(t, par):
                attend, top, prep, end = stages(t)

                def place_max(half):
                    wait_batch_alone(sp, a_free[MAX_T[half] % RING], t, 1 - half, A_TURNS, MAX_T[half] // RING + 1)
                    dst = q_stack[(1 + half + par) % 2][KS:KM, half * HALF:(half + 1) * HALF, :]
                    sp.dma_start(dst.rearrange("o h (i q) -> o (h i) q", q=P).bitcast(F32),
                                 max_t[half][:].bitcast(F32)).then_inc(max_landed[half], DMA)

                if attend:
                    place_max(1)
                if top:
                    wait_batch_alone(sp, f_free, t, 1, F_UNITS, 9)
                    wait_batch_alone(sp, pv_done, t, -1, STEPS, STEPS)
                    sp.dma_start(lat[1 - par][:], lat_staged[:]).then_inc(lat_landed, DMA)
                if end:
                    wait_batch_alone(sp, x1_saved[1 - par], t, -1, *nth(1 - par))
                    wait_batch_alone(sp, t_free, t, -2, T_UNITS, 1)
                    sp.dma_start(x1_back[:], out_tiles[t - 1]).then_inc(x1_loaded, DMA)
                if not isinstance(t, int) or t + 3 < B:
                    wait_batch_alone(sp, f_normed, t, 1, 2, 1)
                    wait_batch_alone(sp, xb_made, t, 1, 1, 1)
                    sp.dma_start(x_in[:, 1 - par], x_tiles[t + 3]).then_inc(x_loaded[1 - par], DMA)
                if prep:
                    wait_batch_alone(sp, f_free, t, 2, F_UNITS, 2)
                    sp.dma_start(out_tiles[t + 2], x1[:, par]).then_inc(x1_saved[par], DMA)
                def stack_queries(half):
                    wait_batch_alone(sp, f_free, t, 2, F_UNITS, 3 + 2 * (half + 1))
                    wait_batch_alone(sp, s_full, t, 0, SCORES, SCORES // 2 * (half + 1))
                    g0 = 2 * half
                    for e in range(HG):
                        for part, src in enumerate((q_high, q_high, q_low)):
                            dst = q_stack[par][part * LD:(part + 1) * LD, g0 * HG:(g0 + 2) * HG, :]
                            dst = dst.rearrange("c (g e) l -> c g e l", e=HG)[:, :, e, :]
                            sp.dma_start(dst.bitcast(F32), src[e * LD:(e + 1) * LD, g0:g0 + 2, :].bitcast(F32)).then_inc(q_stacked[half], DMA)

                if prep:
                    stack_queries(0)
                if top:
                    place_max(0)
                if end:
                    wait_batch_alone(sp, t_free, t, -1, T_UNITS, 3)
                    sp.dma_start(out_tiles[t - 1], x3[:]).then_inc(out_stored, DMA)
                if prep:
                    wait_batch_alone(sp, f_free, t, 2, F_UNITS, 8)
                    wait_batch_alone(sp, s_full, t, 0, SCORES, SCORES)
                    sp.dma_start(keys[par][0:KS, :].bitcast(F32), keys_staged[:].bitcast(F32)).then_inc(keys_landed, DMA)
                    stack_queries(1)

            rounds(sp, one_round)
            sp.wait_ge(out_stored, DMA * B)
            for saved in x1_saved:
                sp.wait_ge(saved, DMA * B // 2)

        @block.gpsimd
        def _(pool):
            nc.gpsimd.memset(identity[:], 0.0).then_inc(const_made, 1)
            nc.gpsimd.memset(ones[:], 1.0).then_inc(const_made, 1)
            nc.gpsimd.memset(neg_half[:], -0.5).then_inc(const_made, 1)
            nc.gpsimd.memset(corner[:], 0.0).then_inc(const_made, 1)
            nc.gpsimd.memset(group_ones[:], 0.0).then_inc(const_made, 1)
            pool.wait_ge(const_made, 7)
            nc.gpsimd.affine_select(out=identity[:], in_=identity[:], compare_op=ALU.not_equal, fill=1.0, base=0,
                                    pattern=[[-1, P]], channel_multiplier=1).then_inc(const_made, 1)
            nc.gpsimd.affine_select(out=corner[:, L - P:], in_=corner[:, L - P:], compare_op=ALU.is_ge, fill=MASKED, base=0,
                                    pattern=[[-1, P]], channel_multiplier=1).then_inc(const_made, 1)
            for g in range(G):
                nc.gpsimd.memset(group_ones[:, g, g::G], 1.0).then_inc(const_made, 1)
                pool.wait_ge(const_made, 10 + g)
            pool.wait_ge(w_dve, 1)

            def one_round(t, par):
                attend, top, prep, end = stages(t)

                def scale_and_bias(moments, per, off, mv, var, rstd, shift, chain, links, done):
                    wait_batch_alone(pool, moments, t, off, per, per)
                    nc.gpsimd.tensor_scalar(var, mv[:, :, 1], EPS, None, ALU.add).then_inc(chain, 1)
                    nc.gpsimd.tensor_scalar(shift[:, 0], mv[:, :, 0], -1.0, None, ALU.mult).then_inc(chain, 1)
                    wait_batch(pool, chain, t, off, links, links - 1)
                    nc.gpsimd.tensor_tensor(rstd, var, neg_half[:], ALU.pow).then_inc(chain, 1)
                    wait_batch(pool, chain, t, off, links, links)
                    nc.gpsimd.tensor_tensor(shift[:, 1], shift[:, 0], rstd, ALU.mult).then_inc(done, 1)

                def scale_y(g):
                    wait_batch(pool, den_made, t, -1, TT + G, TT + 1 + g)
                    if g == 0:
                        wait_batch(pool, y_free, t, -1, G, G)
                    nc.gpsimd.tensor_tensor(y_norm[:, g, :], y_sb[:, g, :], y_norm[:, g, :], ALU.mult).then_inc(y_normed, 1)

                for s in range(STEPS):
                    if prep and s == 0:
                        wait_batch_alone(pool, f_moments, t, 2, 2, 1)
                        nc.gpsimd.tensor_scalar(f_var[:, 0], f_mv[:, 0, :, 1], EPS, None, ALU.add).then_inc(f_pool, 1)
                        wait_batch(pool, f_pool, t, 2, 4, 1)
                        nc.gpsimd.tensor_tensor(f_rstd[:, 0], f_var[:, 0], neg_half[:], ALU.pow).then_inc(f_rstd_made, 1)
                        wait_batch(pool, f_free, t, 1, F_UNITS, 2)
                        nc.gpsimd.tensor_tensor(xb[:], x_in[:, par], half_bias[:, None, :].broadcast_to([P, TT, D]),
                                                ALU.add).then_inc(xb_made, 1)
                    if prep and s == FRONT_AT[1] + 2:
                        wait_batch(pool, f_normed, t, 1, 2, 2)
                        scale_and_bias(f_moments, 2, 2, f_mv[:, 1], f_var[:, 1], f_rstd[:, 1], f_shift,
                                       f_pool, 4, f_rstd_made)
                    if end and s == LAG + 3:
                        scale_y(0)
                        scale_y(1)
                    if end and s == LAG + 4:
                        scale_y(2)
                        scale_y(3)
                    if end and s == TAIL_AT[0] + 2:
                        wait_batch(pool, t_normed, t, -2, 1, 1)
                        scale_and_bias(t_moments, 1, -1, t_mv, t_var[:], t_rstd[:], t_shift, t_pool, 3, t_rstd_made)
                    if attend:
                        n = min(P, L)
                        wait_batch_alone(pool, exp_done, t, 0, SCORES, score_unit(s, HG - 1) + 1)
                        diag = probs[s % BUFS][:, :, 0:n]
                        nc.gpsimd.affine_select(out=diag, in_=diag, compare_op=ALU.is_ge, fill=0.0, base=0,
                                                pattern=[[0, HG], [1, n]], channel_multiplier=-1).then_inc(p_ready, 1)
                    if end and s == TAIL_AT[1]:
                        wait_batch(pool, t_free, t, -1, T_UNITS, 1)
                        nc.gpsimd.tensor_tensor(x2b[:], x2[:], half_bias[:, None, :].broadcast_to([P, TT, D]),
                                                ALU.add).then_inc(x2b_made, 1)

            rounds(pool, one_round)

        @block.scalar
        def _(act):
            def one_round(t, par):
                attend, top, prep, end = stages(t)

                def read_max(half):
                    v = MAX_T[half]
                    wait_batch(act, a_full, t, 1 - half, A_UNITS, v + 1)
                    wait_batch(act, max_landed[half], t, 1 - half, DMA, 0)
                    nc.scalar.activation(max_t[half][:], ring[v % RING][0:MAX_TILES, 0:P], ACT.Copy,
                                         scale=-1.0).then_inc(a_free[v % RING], 1)

                def exp(s, e):
                    n, heads = L - P * (s % TT), SHARED[s % TT]
                    if e % heads:
                        return
                    u = score_unit(s, e)
                    wait_batch(act, s_full, t, 0, SCORES, u + 1)
                    if e == 0:
                        wait_batch(act, pv_done, t, 0, STEPS, s - BUFS + 1)
                    nc.scalar.activation(probs[s % BUFS][:, e:e + heads, 0:n],
                                         scores[u % 2][:, 0:heads * n].rearrange("p (e q) -> p e q", e=heads),
                                         ACT.Exp).then_inc(exp_done, 1)

                def read_y(off, g):
                    wait_batch(act, y_full, t, off, G, g + 1)
                    wait_batch(act, y_normed, t, off - 1, G, g + 1)
                    nc.scalar.activation(y_sb[:, g, :], y_bank[:], ACT.Copy).then_inc(y_free, 1)

                def normalise(dst, src, rstd, shift, tiles):
                    for i in tiles:
                        last = nc.scalar.activation(dst[:, i, :], src[:, i, :], ACT.Identity, bias=shift[:, 1, i:i + 1],
                                                    scale=rstd[:, i:i + 1])
                    return last

                for s in range(STEPS):
                    if attend:
                        exp(s, 0)
                    if prep and s == FRONT_AT[2]:
                        wait_batch(act, f_full, t, 2, F_UNITS, 1)
                        wait_batch(act, f_rstd_made, t, 2, 2, 2)
                        normalise(xn, x1[:, par], f_rstd[:, 1], f_shift, range(TT // 2))
                    if end and s == TAIL_AT[1]:
                        wait_batch(act, t_rstd_made, t, -1, 1, 1)
                        normalise(xn3, x2, t_rstd, t_shift, range(TT // 2))
                    if s == LAG and end:
                        wait_batch(act, pv_done, t, -1, STEPS, STEPS)
                        nc.scalar.activation(den[:], den_bank[:], ACT.Copy).then_inc(den_free, 1)
                    if s == 1 and attend:
                        read_max(1)
                    if top and s and MAX_T[0] in units_of(s - 1):
                        read_max(0)
                    if attend:
                        exp(s, 1)
                    if end and s - 1 == TAIL_AT[1]:
                        wait_batch(act, t_full, t, -1, T_UNITS, 2)
                        nc.scalar.activation(xn3_t[:], aux[:], ACT.Copy).then_inc(t_free, 1)
                    if prep and s - 1 in FRONT_AT:
                        u = FRONT_AT.index(s - 1)
                        wait_batch(act, f_full, t, 2, F_UNITS, u + 1)
                        if u in (0, 2):
                            nc.scalar.activation(xn_t[:], front_bank(t, u)[:], ACT.Copy).then_inc(f_free, 1)
                        elif 3 <= u < 3 + G:
                            wait_batch(act, q_stacked[(u - 3) // 2], t, 2, Q_DMAS * DMA, 0)
                            nc.scalar.activation(q_high[:, u - 3, :], front_bank(t, u)[:], ACT.Copy).then_inc(qh_made, 1)
                        elif u == 3 + G:
                            wait_batch(act, keys_landed, t, 2, DMA, 0)
                            nc.scalar.activation(keys_staged[:], front_bank(t, u)[0:KS, :], ACT.Copy).then_inc(kh_made, 1)
                        elif u == 4 + G:
                            wait_batch(act, lat_landed, t, 2, DMA, 0)
                            nc.scalar.activation(lat_staged[:].rearrange("p i c -> p (i c)"), front_bank(t, u)[:, 0:TT * LD],
                                                 ACT.Copy).then_inc(f_free, 1)
                    if prep and s == FRONT_AT[2]:
                        normalise(xn, x1[:, par], f_rstd[:, 1], f_shift, range(TT // 2, TT)).then_inc(f_normed, 1)
                    if end and s == TAIL_AT[1]:
                        normalise(xn3, x2, t_rstd, t_shift, range(TT // 2, TT)).then_inc(t_normed, 1)
                    if attend:
                        exp(s, 2)
                    if s == LAG - 1 and end:
                        read_y(-1, G - 1)
                    if s >= LAG and (s - LAG + 1) % TT == 0 and attend:
                        read_y(0, (s - LAG) // TT)
                    if attend:
                        exp(s, 3)

            rounds(act, one_round)

        @block.tensor
        def _(pe):
            pe.wait_ge(ffn_loaded, 4 * DMA)
            pe.wait_ge(const_made, 9 + G)
            nc.tensor.transpose(score0[0:RANK, 0:P], a_in[:], identity[:])
            pe.wait_ge(w_dve, 2)
            nc.tensor.transpose(score1[0:1, 0:P], absmax[:, 0:1], identity[:]).then_inc(w_pe, 1)
            pe.wait_ge(w_loaded, 7 * DMA)
            for j in range(H // 2):
                nc.tensor.transpose(ring[j // 4][:, (j % 4) * P:(j % 4 + 1) * P], wq_in[:, j * P:(j + 1) * P], identity[:])
                nc.tensor.transpose(ring[2][:, j * LD:(j + 1) * LD], wk_in[:, j * P:(j + 1) * P], identity[0:LD, 0:LD])
                last = nc.tensor.transpose(aux[:, j * LD:(j + 1) * LD], wv_in[:, j * P:(j + 1) * P], identity[0:LD, 0:LD])
            last.then_inc(w_pe, 1)
            pe.wait_ge(w_dve, 3)
            nc.tensor.matmul(score0[:, 0:D], a_t[:], b_in[:], start=True, stop=True)
            nc.tensor.matmul(score1[:, 0:1], ones[0:1, :], absmax[0:1, 2:3], start=True, stop=True).then_inc(w_pe, 1)
            pe.wait_ge(w_dve, 4)
            for odd, (q_bank, o_bank) in enumerate(((ring[0], y_bank), (ring[1], den_bank))):
                rows = slice(odd * HD, (odd + 1) * HD)
                for j in range(H // 2):
                    e, g = (2 * j + odd) % HG, (2 * j + odd) // HG
                    nc.tensor.matmul(q_bank[:, j * LD:(j + 1) * LD], wq_t[rows, j, :], wk_t[rows, j, :],
                                     start=True, stop=True)
                    last = nc.tensor.matmul(o_bank[e * LD:(e + 1) * LD, g * D:(g + 1) * D], wv_t[rows, j, :],
                                            wout_in[rows, j, :], start=True, stop=True)
            last.then_inc(w_pe, 1)
            pe.wait_ge(w_dve, 5)

            def one_round(t, par):
                attend, top, prep, end = stages(t)

                def score(s, e):
                    g, j = divmod(s, TT)
                    n, heads = L - P * j, SHARED[j]
                    if e % heads:
                        return
                    u = score_unit(s, e)
                    if e == 0 and j == 0 and g % 2 == 0:
                        wait_batch(pe, max_landed[g // 2], t, 0, DMA, DMA)
                    wait_batch(pe, exp_done, t, 0, SCORES, u - 1)
                    for i in range(heads):
                        last = nc.tensor.matmul(scores[u % 2][:, i * n:(i + 1) * n], keys[par][:, j * P:(j + 1) * P],
                                                q_stack[par][:, g * HG + e + i, j * P:L], start=True, stop=True)
                    last.then_inc(s_full, 1)

                def weigh_latents(off, s):
                    g, j = divmod(s, TT)
                    wait_batch(pe, p_ready, t, off, STEPS, s + 1)
                    if s == 0:
                        wait_batch(pe, lat_landed, t, off, DMA, DMA)
                    if j == 0:
                        wait_batch(pe, y_free, t, off, G, g)
                    for e in range(HG):
                        last = nc.tensor.matmul(y_bank[e * LD:(e + 1) * LD, j * P:L], lat[(par + off) % 2][:, j, :],
                                         probs[s % BUFS][:, e, 0:L - P * j], start=(j == 0), stop=(j == TT - 1))
                    if j == TT - 1:
                        last.then_inc(y_full, 1)

                def weigh_ones(off, s):
                    g, j = divmod(s, TT)
                    if s == 0:
                        wait_batch(pe, den_free, t, off, 1, 0)
                    for e in range(HG):
                        last = nc.tensor.matmul(den_bank[e * LD:(e + 1) * LD, j * P:L], group_ones[:, g, :],
                                                probs[s % BUFS][:, e, 0:L - P * j], start=(s == 0), stop=(s == STEPS - 1))
                    last.then_inc(pv_done, 1)

                def max_unit(v):
                    half, i = A_ORDER[v]
                    off, bank = 1, ring[v % RING]
                    if v == MAX_T[1]:
                        off = 0
                    wait_batch(pe, a_free[v % RING], t, off, A_TURNS, v // RING)
                    if i is None:
                        for w in (v - 1, v - 2) if half else ():
                            wait_batch(pe, a_free[w % RING], t, off, A_TURNS, w // RING + 1)
                        nc.tensor.transpose(bank[0:MAX_TILES, 0:P], maxima[:, half * MAX_TILES:(half + 1) * MAX_TILES],
                                            identity[:]).then_inc(a_full, 1)
                        return
                    if i == 0:
                        wait_batch(pe, q_stacked[half], t, 1, Q_DMAS * DMA, Q_DMAS * DMA)
                        if half == 0:
                            wait_batch(pe, keys_landed, t, 1, DMA, DMA)
                    h, j = half * HALF + i // TT, i % TT
                    nc.tensor.matmul(bank[:, 0:P * (j + 1)], q_stack[1 - par][0:KS, h, j * P:(j + 1) * P],
                                     keys[1 - par][0:KS, 0:P * (j + 1)], start=True, stop=True).then_inc(a_full, 1)

                def front_unit(u):
                    bank = front_bank(t, u)
                    if is_first(t) and 3 <= u <= 3 + G:
                        pe.wait_ge(w_dve, 6)
                        pe.wait_ge(f_free, 3)
                    else:
                        wait_batch(pe, f_free, t, 2, F_UNITS, u)
                    turns = sum(s <= FRONT_AT[u] for s in TAIL_AT)
                    if end:
                        wait_batch(pe, t_free, t, -1, T_UNITS, turns)
                    if u in (0, 2):
                        wait_batch(pe, f_normed, t, 2, 2, 1 + u // 2)
                        for i in range(TT):
                            last = nc.tensor.transpose(bank[:, i * P:(i + 1) * P], xn[:, i, :], identity[:])
                    elif u == 1:
                        for i in range(TT):
                            last = nc.tensor.matmul(bank[:, i * D:(i + 1) * D], xn_t[:, i * P:(i + 1) * P], w_ffn[:],
                                                    start=True, stop=True)
                    elif u < 7:
                        w = w_query[:, 2 * (u - 3):2 * (u - 2)].rearrange("p j e c -> p (j e c)")
                        last = nc.tensor.matmul(bank[:], w, xn_t[:], start=True, stop=True)
                    elif u == 7:
                        last = nc.tensor.matmul(bank[0:KS, :], wkv3[:].rearrange("p r c -> p (r c)"), xn_t[:],
                                                start=True, stop=True)
                    else:
                        for i in range(TT):
                            last = nc.tensor.matmul(bank[:, i * LD:(i + 1) * LD], xn_t[:, i * P:(i + 1) * P],
                                                    wkv3[:, 0, :], start=True, stop=True)
                    last.then_inc(f_full, 1)

                def tail_waits(u):
                    wait_batch(pe, t_free, t, -1, T_UNITS, u)
                    if prep:
                        turns = sum(s < TAIL_AT[u] for s in FRONT_AT)
                        wait_batch(pe, f_free, t, 2, F_UNITS, turns)
                    elif u == 0:
                        pe.wait_ge(f_free, F_UNITS * B)

                def project_out(i):
                    if i == 0:
                        tail_waits(0)
                        wait_batch(pe, y_normed, t, -1, G, G)
                    for g in range(G):
                        last = nc.tensor.matmul(aux[:, i * D:(i + 1) * D], y_norm[:, g, i * P:(i + 1) * P],
                                                w_out[:, g, :], start=(g == 0), stop=(g == G - 1))
                    if i == TT - 1:
                        last.then_inc(t_full, 1)

                def tail_unit(u):
                    tail_waits(u)
                    if u == 1:
                        wait_batch(pe, t_normed, t, -1, 1, 1)
                        for i in range(TT):
                            last = nc.tensor.transpose(aux[:, i * P:(i + 1) * P], xn3[:, i, :], identity[:])
                    else:
                        for i in range(TT):
                            last = nc.tensor.matmul(aux[:, i * D:(i + 1) * D], xn3_t[:, i * P:(i + 1) * P], w_ffn[:],
                                                    start=True, stop=True)
                    last.then_inc(t_full, 1)

                for s in range(STEPS):
                    tiles = units_of(s) if top else []
                    slots = 6 + (TT if s == TAIL_AT[0] else 0)

                    def max_units(slot):
                        for n, v in enumerate(tiles):
                            if n * slots // len(tiles) == slot:
                                max_unit(v)

                    off, back = (0, s - LAG) if s >= LAG else (-1, s - LAG + STEPS)
                    weigh = attend if s >= LAG else end
                    if attend:
                        score(s, 0)
                    max_units(0)
                    if attend:
                        score(s, 1)
                    max_units(1)
                    if weigh:
                        weigh_latents(off, back)
                    max_units(2)
                    if attend:
                        score(s, 2)
                    max_units(3)
                    if weigh:
                        weigh_ones(off, back)
                    max_units(4)
                    if attend:
                        score(s, 3)
                        if s == 0:
                            max_unit(MAX_T[1])
                    max_units(5)
                    if end and s in TAIL_AT[1:]:
                        tail_unit(TAIL_AT.index(s))
                    if s == TAIL_AT[0]:
                        for i in range(TT):
                            if end:
                                project_out(i)
                            max_units(6 + i)
                    if prep and s in FRONT_AT:
                        front_unit(FRONT_AT.index(s))

            rounds(pe, one_round)

        @block.vector
        def _(dve):
            nc.vector.memset(keys[0][KS:KM, :].bitcast(F32), 1.0).then_inc(const_made, 1)
            nc.vector.memset(keys[1][KS:KM, :].bitcast(F32), 1.0).then_inc(const_made, 1)
            dve.wait_ge(ffn_loaded, 4 * DMA)
            nc.vector.tensor_scalar(half_bias[:], half_bias[:], 0.5, None, ALU.mult).then_inc(w_dve, 1)
            nc.vector.tensor_reduce(absmax[:, 0:1], ffn_in[:], AX.X, ALU.max, apply_absolute_value=True).then_inc(w_dve, 1)
            dve.wait_ge(x_loaded[0], DMA)
            for i in range(TT):
                last = nc.vector.bn_stats(f_stats[:, 0, i, :], x_in[:, 0, i, :])
            last.then_inc(f_dve, 1)
            dve.wait_ge(f_dve, 1)
            for i in range(TT):
                last = nc.vector.bn_aggr(f_mv[:, 0, i, :], f_stats[:, 0, i, :])
            last.then_inc(f_moments, 1)
            chain = [0]

            def link(ins):
                chain[0] += 1
                ins.then_inc(w_chain, 1)
                dve.wait_ge(w_chain, chain[0])

            dve.wait_ge(w_pe, 1)
            nc.vector.tensor_copy(a_t[:], score0[0:RANK, 0:P])
            link(nc.vector.tensor_reduce(absmax[0:1, 1:2], score1[0:1, 0:P], AX.X, ALU.max))
            nc.vector.tensor_scalar(absmax[0:1, 2:3], absmax[0:1, 1:2], 1.0 / QMAX, None, ALU.mult).then_inc(w_dve, 1)
            dve.wait_ge(w_pe, 2)
            for i in range(2):
                nc.vector.tensor_copy(wq_t[:, i * 4:(i + 1) * 4, :].rearrange("p j d -> p (j d)"), ring[i][:])
            nc.vector.tensor_copy(wk_t[:].rearrange("p j c -> p (j c)"), ring[2][:, 0:H // 2 * LD])
            nc.vector.tensor_copy(wv_t[:].rearrange("p j c -> p (j c)"), aux[:, 0:H // 2 * LD]).then_inc(w_dve, 1)
            dve.wait_ge(w_pe, 3)
            link(nc.vector.tensor_copy(absmax[:, 3:4], score1[:, 0:1]))
            link(nc.vector.reciprocal(absmax[:, 1:2], absmax[:, 3:4]))
            link(nc.vector.tensor_scalar(quant[:, 0], ffn_in[:], absmax[:, 1:2], ROUND, ALU.mult, ALU.add))
            link(nc.vector.tensor_scalar(quant[:, 1], quant[:, 0], -ROUND, QMAX, ALU.add, ALU.min))
            link(nc.vector.tensor_scalar(quant[:, 0], quant[:, 1], -QMAX - 1.0, absmax[:, 3:4], ALU.max, ALU.mult))
            link(nc.vector.tensor_tensor(quant[:, 1], score0[:, 0:D], quant[:, 0], ALU.add))
            nc.vector.tensor_scalar(w_ffn[:], quant[:, 1], 0.5, None, ALU.mult).then_inc(w_dve, 1)
            dve.wait_ge(f_rstd_made, 1)
            for i in range(TT):
                last = nc.vector.tensor_scalar(xn[:, i, :], x_in[:, 0, i, :], f_mv[:, 0, i, 0:1], f_rstd[:, 0, i:i + 1],
                                               ALU.subtract, ALU.mult)
            last.then_inc(f_normed, 1)
            dve.wait_ge(w_pe, 4)
            for odd, (q_bank, o_bank) in enumerate(((ring[0], y_bank), (ring[1], den_bank))):
                last = nc.vector.tensor_scalar(w_query[:, :, odd, :],
                                               q_bank[:, 0:H // 2 * LD].rearrange("p (j c) -> p j c", c=LD),
                                               HD ** -0.5, None, ALU.mult)
                for e in (odd, odd + 2):
                    rows = slice(e * LD, (e + 1) * LD)
                    last = nc.vector.tensor_copy(w_out[rows].rearrange("p g o -> p (g o)"), o_bank[rows, :])
            last.then_inc(w_dve, 1)

            def one_round(t, par):
                attend, top, prep, end = stages(t)

                def statistics(src, stats, chain):
                    for i in range(TT):
                        last = nc.vector.bn_stats(stats[:, i, :], src[:, i, :])
                    last.then_inc(chain, 1)

                def moments(stats, mv, chain, per, k, off, done):
                    wait_batch_alone(dve, chain, t, off, per, k)
                    for i in range(TT):
                        last = nc.vector.bn_aggr(mv[:, i, :], stats[:, i, :])
                    last.then_inc(done, 1)

                def max_unit(v):
                    half, i = A_ORDER[v]
                    if i is None:
                        return
                    h, j = half * HALF + i // TT, i % TT
                    n = P * (j + 1)
                    wait_batch_alone(dve, a_full, t, 1, A_UNITS, v + 1)
                    bank = ring[v % RING][:, 0:n]
                    nc.vector.tensor_tensor_reduce(out=bank, in0=bank, in1=corner[:, L - n:],
                                                   scale=1.0, scalar=MASKED, op0=ALU.add, op1=ALU.max,
                                                   accum_out=maxima[:, h * TT + j:h * TT + j + 1]).then_inc(a_free[v % RING], 1)

                def invert(k):
                    if k == 0:
                        wait_batch(dve, den_free, t, -1, 1, 1)
                    part = slice(k * P, (k + 1) * P)
                    nc.vector.reciprocal(den_inv[:, part], den[:, part]).then_inc(den_made, 1)

                def spread(g):
                    if g == 0:
                        wait_batch_alone(dve, den_made, t, -1, TT + G, TT)
                    nc.vector.stream_shuffle(y_norm[:, g, :], den_inv[:], [g] * LD).then_inc(den_made, 1)

                for s in range(STEPS):
                    tiles = units_of(s) if top else []
                    for v in tiles[:1]:
                        max_unit(v)
                    if prep and s == 0 and not is_first(t):
                        wait_batch(dve, x_loaded[par], t, 2, *nth(par))
                        statistics(x_in[:, par], f_stats[:, 0], f_dve)
                        moments(f_stats[:, 0], f_mv[:, 0], f_dve, 2, 1, 2, f_moments)
                    if prep and s == 1 and not is_first(t):
                        wait_batch(dve, f_rstd_made, t, 2, 2, 1)
                        wait_batch(dve, f_full, t, 1, F_UNITS, 3)
                        for i in range(TT):
                            last = nc.vector.tensor_scalar(xn[:, i, :], x_in[:, par, i, :], f_mv[:, 0, i, 0:1],
                                                           f_rstd[:, 0, i:i + 1], ALU.subtract, ALU.mult)
                        last.then_inc(f_normed, 1)
                    if prep and s == FRONT_AT[1] + 1:
                        wait_batch(dve, f_full, t, 2, F_UNITS, 2)
                        wait_batch(dve, xb_made, t, 2, 1, 1)
                        wait_batch(dve, x1_saved[par], t, 0, *nth(par))
                        nc.vector.tensor_tensor(x1[:, par].rearrange("p i d -> p (i d)"), aux[:],
                                                xb[:].rearrange("p i d -> p (i d)"), ALU.add).then_inc(f_free, 1)
                    if end:
                        if s == LAG:
                            invert(0)
                        elif s == LAG + 2:
                            invert(3)
                        elif s == LAG + 3:
                            spread(2)
                        elif s == TAIL_AT[0] + 1:
                            wait_batch(dve, t_full, t, -1, T_UNITS, 1)
                            wait_batch(dve, x1_loaded, t, -1, DMA, DMA)
                            nc.vector.tensor_tensor(x2[:].rearrange("p i d -> p (i d)"), aux[:],
                                                    x1_back[:].rearrange("p i d -> p (i d)"), ALU.add).then_inc(t_free, 1)
                        elif s == TAIL_AT[2] + 1:
                            wait_batch(dve, t_full, t, -1, T_UNITS, 3)
                            wait_batch(dve, x2b_made, t, -1, 1, 1)
                            wait_batch(dve, out_stored, t, -1, DMA, 0)
                            nc.vector.tensor_tensor(x3[:].rearrange("p i d -> p (i d)"), aux[:],
                                                    x2b[:].rearrange("p i d -> p (i d)"), ALU.add).then_inc(t_free, 1)
                    for v in tiles[1:2]:
                        max_unit(v)
                    if prep and s - 1 in FRONT_AT[3:3 + G]:
                        g = FRONT_AT.index(s - 1) - 3
                        wait_batch(dve, qh_made, t, 2, G, g + 1)
                        nc.vector.tensor_tensor(q_low[:, g, :], front_bank(t, 3 + g)[:], q_high[:, g, :].bitcast(F32),
                                                ALU.subtract).then_inc(f_free, 1)
                    if prep and s == FRONT_AT[3 + G] + 1:
                        wait_batch(dve, kh_made, t, 2, 1, 1)
                        low = keys_staged[LD:2 * LD, :]
                        nc.vector.tensor_tensor(low, front_bank(t, 3 + G)[LD:2 * LD, :], low.bitcast(F32),
                                                ALU.subtract).then_inc(f_free, 1)
                    if prep and s == FRONT_AT[1] + 1:
                        wait_batch(dve, f_free, t, 2, F_UNITS, 2)
                        statistics(x1[:, par], f_stats[:, 1], f_dve)
                    if end and s == TAIL_AT[0] + 1:
                        wait_batch(dve, t_free, t, -1, T_UNITS, 1)
                        statistics(x2, t_stats, t_dve)
                    if end and s == LAG + 2:
                        spread(0)
                    if end and s == LAG + 3:
                        spread(3)
                    for v in tiles[2:3]:
                        max_unit(v)
                    if prep and s == FRONT_AT[1] + 1:
                        moments(f_stats[:, 1], f_mv[:, 1], f_dve, 2, 2, 2, f_moments)
                    if end and s == TAIL_AT[0] + 1:
                        moments(t_stats, t_mv, t_dve, 1, 1, -1, t_moments)
                    if end and s == LAG:
                        invert(1)
                    if end and s == LAG + 2:
                        spread(1)
                    for v in tiles[3:4]:
                        max_unit(v)
                    if end and s == LAG + 1:
                        invert(2)
                    for v in tiles[4:]:
                        max_unit(v)

            rounds(dve, one_round)


_INS = ['L0_attn_x_bld', 'L0_attn_Wq', 'L0_attn_Wkv_down', 'L0_attn_Wk_up', 'L0_attn_Wv_up', 'L0_attn_Wout',
        'L0_ffn_kernel', 'L0_ffn_bias', 'L0_ffn_a', 'L0_ffn_b']
_OUTS = [((16, 512, 128), 'float32')]


def kernel(**inputs):
    import numpy as _np
    import concourse.bacc as _bacc
    from concourse import mybir as _mybir
    from concourse.bass_utils import run_bass_kernel_spmd as _run

    nc = _bacc.Bacc("TRN2", target_bir_lowering=False, num_devices=1)
    arrays, args = {}, []
    for name in _INS:
        a = _np.ascontiguousarray(inputs[name])
        arrays[f"in_{name}_dram"] = a
        args.append(nc.dram_tensor(f"in_{name}_dram", a.shape, _mybir.dt.from_np(a.dtype), kind="ExternalInput").ap())
    for i, (shape, dtype) in enumerate(_OUTS):
        dt = _mybir.dt.from_np(_np.dtype(dtype))
        args.append(nc.dram_tensor(f"out_{i}_dram", shape, dt, kind="ExternalOutput").ap())
    macaron_block(nc, *args)
    r = _run(nc, [arrays], core_ids=[0])
    got = tuple(r.results[0][f"out_{i}_dram"] for i in range(len(_OUTS)))
    return got[0]
```
